# Optimizing a Trainium2 kernel written in Bass

```python
import numpy as np
import jax
import jax.numpy as jnp

def _softmax(x, axis=-1):
    return jax.nn.softmax(x, axis=axis)

def _gelu(x):
    return jax.nn.gelu(x, approximate=True)

def _silu(x):
    return jax.nn.silu(x)

def _sigmoid(x):
    return jax.nn.sigmoid(x)

def _layernorm(x, axis=-1, eps=1e-05):
    m = jnp.mean(x, axis=axis, keepdims=True)
    v = jnp.var(x, axis=axis, keepdims=True)
    return (x - m) / jnp.sqrt(v + eps)

def _scatter_add(tgt, idx, src, axis=0):
    return tgt.at[idx].add(src)

def _segment_sum(src, seg, n):
    return jax.ops.segment_sum(src, seg, n)
kernel_name = 'mk_gnn_resnorm_d4_gnn_r32_14f152'

def setup_inputs(seed: int=0):
    np.random.seed(seed)
    _w = jnp.asarray

    def _rec_inputs():
        import jax
        import jax.numpy as jnp
        _gk = jax.random.key(seed)
        x = -0.0001006 + 1 * jax.random.normal(jax.random.fold_in(_gk, 1), (3125, 96), jnp.float32)
        _s = jax.random.randint(jax.random.fold_in(_gk, 2), (50000,), 0, 3125, jnp.int32)
        _d = jax.random.randint(jax.random.fold_in(_gk, 3), (50000,), 0, 3125, jnp.int32)
        _loop = jnp.arange(3125, dtype=jnp.int32)
        src = jnp.concatenate([_s, _d, _loop])
        dst = jnp.concatenate([_d, _s, _loop])
        _o = jnp.argsort(dst, stable=True)
        src = src[_o]
        dst = dst[_o]
        edge_attr_96 = 5.93493e-05 + 1.00006 * jax.random.normal(jax.random.fold_in(_gk, 12), (103125, 96), jnp.float32)
        return (x, src, dst, edge_attr_96)
    x, src, dst, edge_attr_96 = _rec_inputs()

    def _L0_gnn_setup():
        import jax, jax.numpy as jnp
        import numpy as np
        N_NODES = 50000
        N_EDGES = 25000
        D = 96
        key = jax.random.key(seed)
        k_x, k_src, k_dst, k_ws, k_wn = jax.random.split(key, 5)
        x = jax.random.normal(k_x, (N_NODES, D), dtype=jnp.float32)
        src = jax.random.randint(k_src, (N_EDGES,), 0, N_NODES, dtype=jnp.int32)
        dst = jax.random.randint(k_dst, (N_EDGES,), 0, N_NODES, dtype=jnp.int32)
        W_self = jax.random.normal(k_ws, (D, D), dtype=jnp.float32) / np.sqrt(D)
        W_neigh = jax.random.normal(k_wn, (D, D), dtype=jnp.float32) / np.sqrt(D)
        b = jnp.zeros((D,), dtype=jnp.float32)
        return {'x': x, 'src': src, 'dst': dst, 'W_self': W_self, 'W_neigh': W_neigh, 'b': b}
    _L0_gnn_all = _L0_gnn_setup()
    _L0_gnn_in = {k: v for k, v in _L0_gnn_all.items() if k in ('W_self', 'W_neigh', 'b')}
    del _L0_gnn_all

    def _L1_gnn_setup():
        import jax, jax.numpy as jnp
        import numpy as np
        N_NODES = 50000
        N_EDGES = 25000
        IN_DIM = 96
        NUM_HEADS = 8
        HEAD_DIM = IN_DIM // NUM_HEADS
        key = jax.random.key(seed)
        ks = jax.random.split(key, 11)
        s = 1.0 / np.sqrt(IN_DIM)
        return {'x': jax.random.normal(ks[0], (N_NODES, IN_DIM), dtype=jnp.float32), 'edge_index': jax.random.randint(ks[1], (2, N_EDGES), 0, N_NODES, dtype=jnp.int64), 'edge_attr': jax.random.normal(ks[2], (N_EDGES, IN_DIM), dtype=jnp.float32), 'Wq': jax.random.normal(ks[3], (IN_DIM, IN_DIM), dtype=jnp.float32) * s, 'bq': jax.random.normal(ks[4], (IN_DIM,), dtype=jnp.float32) * s, 'Wk': jax.random.normal(ks[5], (IN_DIM, IN_DIM), dtype=jnp.float32) * s, 'bk': jax.random.normal(ks[6], (IN_DIM,), dtype=jnp.float32) * s, 'We': jax.random.normal(ks[7], (IN_DIM, IN_DIM), dtype=jnp.float32) * s, 'be': jax.random.normal(ks[8], (IN_DIM,), dtype=jnp.float32) * s, 'Wv': jax.random.normal(ks[9], (IN_DIM, IN_DIM), dtype=jnp.float32) * s, 'bv': jax.random.normal(ks[10], (IN_DIM,), dtype=jnp.float32) * s}
    _L1_gnn_all = _L1_gnn_setup()
    _L1_gnn_in = {k: v for k, v in _L1_gnn_all.items() if k in ('Wq', 'bq', 'Wk', 'bk', 'We', 'be', 'Wv', 'bv')}
    del _L1_gnn_all

    def _L2_gnn_setup():
        import jax, jax.numpy as jnp
        import numpy as np
        N_NODES = 50000
        N_EDGES = 25000
        IN_FEATS = 96
        OUT_FEATS = 96
        key = jax.random.key(seed)
        k1, k2, k3, k4, k5 = jax.random.split(key, 5)
        feat = jax.random.normal(k1, (N_NODES, IN_FEATS), dtype=jnp.float32)
        weight = jax.random.normal(k2, (IN_FEATS, OUT_FEATS), dtype=jnp.float32) * 0.05
        bias = jax.random.normal(k3, (OUT_FEATS,), dtype=jnp.float32) * 0.05
        src = jax.random.randint(k4, (N_EDGES,), 0, N_NODES, dtype=jnp.int64 if jax.config.jax_enable_x64 else jnp.int32)
        dst = jax.random.randint(k5, (N_EDGES,), 0, N_NODES, dtype=jnp.int64 if jax.config.jax_enable_x64 else jnp.int32)
        return {'feat': feat, 'weight': weight, 'bias': bias, 'src': src, 'dst': dst}
    _L2_gnn_all = _L2_gnn_setup()
    _L2_gnn_in = {k: v for k, v in _L2_gnn_all.items() if k in ('weight', 'bias')}
    del _L2_gnn_all

    def _L3_gnn_setup():
        import jax, jax.numpy as jnp
        import numpy as np
        N_NODES = 50000
        N_EDGES = 25000
        D_IN = 96
        D_OUT = 96
        key = jax.random.key(seed)
        k1, k2, k3, k4, k5, k6 = jax.random.split(key, 6)
        x = jax.random.normal(k1, (N_NODES, D_IN), dtype=jnp.float32)
        edge_index = jax.random.randint(k2, (2, N_EDGES), 0, N_NODES, dtype=jnp.int32)
        W_lin = jax.random.normal(k3, (D_OUT, D_IN), dtype=jnp.float32) * 0.1
        b_lin = jax.random.normal(k4, (D_OUT,), dtype=jnp.float32) * 0.1
        W_root = jax.random.normal(k5, (D_OUT, D_IN), dtype=jnp.float32) * 0.1
        b_root = jax.random.normal(k6, (D_OUT,), dtype=jnp.float32) * 0.1
        return {'x': x, 'edge_index': edge_index, 'W_lin': W_lin, 'b_lin': b_lin, 'W_root': W_root, 'b_root': b_root}
    _L3_gnn_all = _L3_gnn_setup()
    _L3_gnn_in = {k: v for k, v in _L3_gnn_all.items() if k in ('W_lin', 'b_lin', 'W_root', 'b_root')}
    del _L3_gnn_all
    return {'x': x, 'src': src, 'dst': dst, 'edge_attr_96': edge_attr_96, 'L0_gnn_W_self': _L0_gnn_in['W_self'], 'L0_gnn_W_neigh': _L0_gnn_in['W_neigh'], 'L0_gnn_b': _L0_gnn_in['b'], 'L1_gnn_Wq': _L1_gnn_in['Wq'], 'L1_gnn_bq': _L1_gnn_in['bq'], 'L1_gnn_Wk': _L1_gnn_in['Wk'], 'L1_gnn_bk': _L1_gnn_in['bk'], 'L1_gnn_We': _L1_gnn_in['We'], 'L1_gnn_be': _L1_gnn_in['be'], 'L1_gnn_Wv': _L1_gnn_in['Wv'], 'L1_gnn_bv': _L1_gnn_in['bv'], 'L2_gnn_weight': _L2_gnn_in['weight'], 'L2_gnn_bias': _L2_gnn_in['bias'], 'L3_gnn_W_lin': _L3_gnn_in['W_lin'], 'L3_gnn_b_lin': _L3_gnn_in['b_lin'], 'L3_gnn_W_root': _L3_gnn_in['W_root'], 'L3_gnn_b_root': _L3_gnn_in['b_root']}

def reference(x, src, dst, edge_attr_96, L0_gnn_W_self, L0_gnn_W_neigh, L0_gnn_b, L1_gnn_Wq, L1_gnn_bq, L1_gnn_Wk, L1_gnn_bk, L1_gnn_We, L1_gnn_be, L1_gnn_Wv, L1_gnn_bv, L2_gnn_weight, L2_gnn_bias, L3_gnn_W_lin, L3_gnn_b_lin, L3_gnn_W_root, L3_gnn_b_root):
    import jax
    import jax.numpy as jnp

    def _L0_gnn_ref(x, src, dst, W_self, W_neigh, b):
        import jax, jax.numpy as jnp
        import numpy as np
        N_NODES = 50000
        N_EDGES = 25000
        D = 96
        n = x.shape[0]
        msg = x[src]
        neigh_sum = jax.ops.segment_sum(msg, dst, num_segments=n)
        deg = jax.ops.segment_sum(jnp.ones(src.shape, x.dtype), dst, num_segments=n)
        h_neigh = neigh_sum / jnp.maximum(deg, 1.0)[:, None]
        return x @ W_self + h_neigh @ W_neigh + b

    def _L1_gnn_ref(x, edge_index, edge_attr, Wq, bq, Wk, bk, We, be, Wv, bv):
        import jax, jax.numpy as jnp
        import numpy as np
        N_NODES = 50000
        N_EDGES = 25000
        IN_DIM = 96
        NUM_HEADS = 8
        HEAD_DIM = IN_DIM // NUM_HEADS
        N = x.shape[0]
        H, D = (NUM_HEADS, HEAD_DIM)
        Q_h = (x @ Wq + bq).reshape(N, H, D)
        K_h = (x @ Wk + bk).reshape(N, H, D)
        V_h = (x @ Wv + bv).reshape(N, H, D)
        E = (edge_attr @ We + be).reshape(-1, H, D)
        src_idx = edge_index[0]
        dst_idx = edge_index[1]
        src = K_h[src_idx]
        dest = Q_h[dst_idx]
        score = src * dest / jnp.sqrt(jnp.asarray(D, x.dtype))
        score = score * E
        score = jnp.exp(jnp.clip(score.sum(-1, keepdims=True), -5.0, 5.0))
        msg = V_h[src_idx] * score
        wV = jax.ops.segment_sum(msg, dst_idx, num_segments=N)
        Z = jax.ops.segment_sum(score, dst_idx, num_segments=N)
        h_out = wV / (Z + 1e-06)
        return h_out.reshape(N, H * D)

    def _L2_gnn_ref(feat, weight, bias, src, dst):
        import jax, jax.numpy as jnp
        import numpy as np
        N_NODES = 50000
        N_EDGES = 25000
        IN_FEATS = 96
        OUT_FEATS = 96
        N = feat.shape[0]
        ones = jnp.ones(src.shape, dtype=feat.dtype)
        out_deg = jnp.clip(jax.ops.segment_sum(ones, src, num_segments=N), 1.0)
        in_deg = jnp.clip(jax.ops.segment_sum(ones, dst, num_segments=N), 1.0)
        feat_n = feat * (out_deg ** (-0.5))[:, None]
        agg = jax.ops.segment_sum(feat_n[src], dst, num_segments=N)
        rst = agg @ weight
        rst = rst * (in_deg ** (-0.5))[:, None]
        return rst + bias

    def _L3_gnn_ref(x, edge_index, W_lin, b_lin, W_root, b_root):
        import jax, jax.numpy as jnp
        import numpy as np
        N_NODES = 50000
        N_EDGES = 25000
        D_IN = 96
        D_OUT = 96
        src, dst = (edge_index[0], edge_index[1])
        n = x.shape[0]
        deg = jax.ops.segment_sum(jnp.ones(src.shape[0], dtype=x.dtype), dst, num_segments=n)
        dinv = jax.lax.rsqrt(jnp.maximum(deg, 1.0))
        norm = dinv[src] * dinv[dst]
        h = x @ W_lin.T + b_lin
        msgs = h[src] * norm[:, None]
        agg = jax.ops.segment_sum(msgs, dst, num_segments=n)
        out = agg + x @ W_root.T + b_root
        return jax.nn.relu(out)
    edge_index = jnp.stack([src, dst])
    x = _layernorm(x + _L0_gnn_ref(x, src, dst, L0_gnn_W_self, L0_gnn_W_neigh, L0_gnn_b), axis=-1)
    x = _layernorm(x + _L1_gnn_ref(x, edge_index, edge_attr_96, L1_gnn_Wq, L1_gnn_bq, L1_gnn_Wk, L1_gnn_bk, L1_gnn_We, L1_gnn_be, L1_gnn_Wv, L1_gnn_bv), axis=-1)
    x = _layernorm(x + _L2_gnn_ref(x, L2_gnn_weight, L2_gnn_bias, src, dst), axis=-1)
    x = _layernorm(x + _L3_gnn_ref(x, edge_index, L3_gnn_W_lin, L3_gnn_b_lin, L3_gnn_W_root, L3_gnn_b_root), axis=-1)
    return x

_drawn_inputs = setup_inputs


def setup_inputs(seed=0):
    import zlib

    import numpy as np

    out = dict(_drawn_inputs(seed))
    spreads = {'L0_gnn_b': (0.0, 0.1)}
    factors = {}
    for name, (base, spread) in spreads.items():
        noise = np.random.default_rng([zlib.crc32(name.encode()), seed]).standard_normal(out[name].shape)
        drawn = base * np.exp(spread * noise) if base else spread * noise
        out[name] = jnp.asarray(drawn.astype(out[name].dtype))
    for name, factor in factors.items():
        out[name] = (out[name] * factor).astype(out[name].dtype)
    return out
```

```python
import concourse.bass as bass
from concourse import mybir
from contextlib import ExitStack


def residual_gnn_kernel(nc, x_in, src_in, dst_in, ea_in, w_self, w_neigh, w_kvq, w_edge, w_gcn, w_lin_root, out):
    fp32, bf16, i32 = mybir.dt.float32, mybir.dt.bfloat16, mybir.dt.int32
    ALU, ACT, AX = mybir.AluOpType, mybir.ActivationFunctionType, mybir.AxisListType.X

    P = 128
    D = 96
    H = 8
    HD = D // H
    NB = x_in.shape[0] // P
    NR = NB * P
    NT = src_in.shape[1]
    G = 5
    CG = 6
    CT = G * CG
    C = NT // CT
    HT = CT // 2
    KV_RING = 3
    USED0 = KV_RING + 1
    QSCALE = float(HD) ** -0.5
    PAD_DST = 1 << 20
    LAST_BASE = NR - P
    PASSES_MAX = (3125 - 1) // P + 1

    ctx = ExitStack()
    with ctx:
        def sb(name, shape, dt=fp32):
            return ctx.enter_context(nc.sbuf_tensor(name, shape, dt))

        def pb(name, shape, dt=fp32):
            return ctx.enter_context(nc.psum_tensor(name, shape, dt))

        def sem(name):
            return ctx.enter_context(nc.semaphore(name))

        kv_tab = nc.dram_tensor("kv_tab", [NR, 2 * D], fp32, kind="Internal").ap()
        q_tab = nc.dram_tensor("q_tab", [NR, 3 * D], bf16, kind="Internal").ap()
        t2_tab = nc.dram_tensor("t2_tab", [NR, D], fp32, kind="Internal").ap()
        t3_tab = nc.dram_tensor("t3_tab", [NR, D], fp32, kind="Internal").ap()
        WA = D + 1
        WT = D + H
        sums = {0: nc.dram_tensor("sum0", [NR, WA], fp32, kind="Internal").ap(),
                1: nc.dram_tensor("sum1", [NR, WT], fp32, kind="Internal").ap(),
                2: nc.dram_tensor("sum2", [NR, WA], fp32, kind="Internal").ap(),
                3: nc.dram_tensor("sum3", [NR, WA], fp32, kind="Internal").ap()}
        tables = {0: x_in, 2: t2_tab, 3: t3_tab}

        def rows(ap):
            return ap.rearrange("(b p) d -> p b d", p=P)

        ident = sb("ident", [P, P])
        ident_b = sb("ident_b", [P, P], bf16)
        iota_i = sb("iota_i", [P, P], i32)
        iota_f = sb("iota_f", [P, P])
        src_all = sb("src_all", [P, NT], i32)
        dst_all = sb("dst_all", [P, NT], i32)
        dst_f = sb("dst_f", [P, NT])
        slot0 = sb("slot0", [P, NT])
        slot = sb("slot", [P, NT])
        cmin = sb("cmin", [P, 2 * C])
        cred = sb("cred", [C, 2])
        cwide = sb("cwide", [C, 2, P])
        base0 = sb("base0", [P, C])
        base_f = sb("base_f", [1, C])
        base_i = sb("base_i", [1, C + 1], i32)
        span_f = sb("span_f", [1, C])
        span_m = sb("span_m", [1, 1])
        span_i = sb("span_i", [1, 1], i32)

        xa = sb("xa", [P, NB, D])
        ya = sb("ya", [P, NB, D])
        za = sb("za", [P, NB, D])
        agg = sb("agg", [P, NB, WT])
        sq = agg[:, :, 0:D]
        stat = sb("stat", [P, 4, NB])
        outdeg = sb("outdeg", [P, NB])
        indeg = sb("indeg", [P, NB])
        dinv_out = sb("dinv_out", [P, NB])
        dinv_in = sb("dinv_in", [P, NB])
        kvq = sb("kvq", [P, NB, 3 * D])
        qs = sb("qs", [P, NB, 3 * D], bf16)
        r3 = kvq[:, :, D:2 * D]
        t3 = kvq[:, :, 0:D]

        w_self_t = sb("w_self_t", [D + 1, D])
        w_neigh_t = sb("w_neigh_t", [D, D])
        w_kvq_t = sb("w_kvq_t", [D + 1, 3 * D])
        w_edge_t = sb("w_edge_t", [D + 1, D])
        w_gcn_t = sb("w_gcn_t", [D + 1, D])
        w_lr_t = sb("w_lr_t", [D + 1, 2 * D])

        xs = sb("xs", [P, 2, 2 * D])
        xT = sb("xT", [D + 1, 2, 2 * P])

        idx = sb("idx", [P, 2, HT], i32)
        kv = sb("kv", [P, KV_RING, G, 2 * D])
        xg = sb("xg", [P, KV_RING, G, WA])
        ea = sb("ea", [D + 1, KV_RING, G * P])
        oh = sb("oh", [P, 2, G, P])
        oh_b = sb("oh_b", [P, 2, G, P], bf16)
        ohT = sb("ohT", [P, 2, G, P], bf16)
        q_land = sb("q_land", [P, 3 * D], bf16)
        q_win = sb("q_win", [P, 3 * D], bf16)
        prod = sb("prod", [P, 2, G * D])
        sc = sb("sc", [P, 2, G * H])
        msg = sb("msg", [P, 2, G, WT])
        flush = sb("flush", [P, WT])
        zeros = sb("zeros", [P, NB * WT])

        lo_i = sb("lo_i", [P, NT], i32)
        hi_i = sb("hi_i", [P, NT], i32)
        lo_f = sb("lo_f", [P, NT])
        hi_f = sb("hi_f", [P, NT])
        oh_hi = sb("oh_hi", [P, 2, G, NB], bf16)

        bank = [pb(f"bank{i}", [P, 512]) for i in range(8)]
        E_ps = [bank[0], bank[1]]
        Q_ps = [bank[2], bank[3]]
        T_ps = [bank[4][:, :].bitcast(bf16), bank[5][:, :].bitcast(bf16)]
        acc = bank[6]
        N_t = [bank[0], bank[1]]
        N_o = [bank[2], bank[3]]

        s_in_x, s_in_e, s_in_w, s_zeroed = sem("in_x"), sem("in_e"), sem("in_w"), sem("zeroed")
        s_zeros = sem("zeros_ready")
        s_pool = sem("pool_step")
        s_ident = sem("ident_ready")
        s_identb = sem("identb_ready")
        s_prep = sem("prep_step")
        s_prep_pe = sem("prep_transposed")
        s_base = sem("bases_ready")
        s_deg_oh, s_deg_mm = sem("deg_onehot"), sem("deg_summed")

        block = ctx.enter_context(nc.Block())

        class Agg:
            def __init__(self, k):
                n = f"L{k}_"
                self.idx_ready = [sem(n + f"idx_ready{i}") for i in range(2)]
                self.gathered = [sem(n + f"gathered{i}") for i in range(KV_RING)]
                self.used = sem(n + "used")
                self.oh_ready = sem(n + "onehot")
                self.chunk_summed = sem(n + "chunk_summed")
                self.flush_ready = sem(n + "flush_ready")
                self.flushed = sem(n + "flushed")
                self.pass_ready = sem(n + "pass_ready")
                self.go = sem(n + "table_ready")
                self.step = sem(n + "dve_step")

        L = {k: Agg(k) for k in range(4)}
        A = L[1]
        A.q_ready, A.qwin = sem("L1_q_loaded"), sem("L1_q_window")
        A.ea_ready = [sem(f"L1_ea_ready{i}") for i in range(KV_RING)]
        A.e_done, A.ohT_ps, A.ohT_sb, A.q_done = sem("L1_e"), sem("L1_ohT_ps"), sem("L1_ohT_sb"), sem("L1_q")
        A.oh32, A.t1, A.t2, A.red, A.sc, A.exp, A.seg = (sem("L1_oh32"), sem("L1_t1"), sem("L1_t2"), sem("L1_red"),
                                                         sem("L1_scores"), sem("L1_exp"), sem("L1_segment"))

        n_go, n_staged, n_tr, n_xT = sem("node_input"), sem("node_staged"), sem("node_transposed"), sem("node_xT")
        n_mm, n_ev, n_step = sem("node_product"), sem("node_evicted"), sem("node_dve_step")
        s_sqrt_in, s_sqrt = sem("sqrt_input"), sem("sqrt_done")
        s_kvq, s_t2, s_t3, s_final = sem("kvq_ready"), sem("t2_ready"), sem("t3_ready"), sem("final_ready")
        s_stored = sem("stored")
        s_waited = sem("waited")
        sums_whole = [sem(f"sums{k}_whole") for k in range(4)]
        sums_loaded = [sem(f"sums{k}_loaded") for k in range(4)]

        def passes(eng):
            eng.wait_ge(s_base, 1)
            span = eng.value_load(span_i[0:1, 0:1], min_val=0, max_val=3124)
            return eng.snap(span // P + 1, min_val=1, max_val=PASSES_MAX)

        def wait_alone(eng, s, value):
            eng.wait_ge(s, value)
            eng.sem_inc(s_waited, 1)

        @block.sync
        def _(sp):
            sp.dma_start(dst_all[:, :], dst_in).then_inc(s_in_e, 16)
            sp.dma_start(src_all[:, :], src_in).then_inc(s_in_e, 16)
            sp.dma_start(xa[:, :, :], rows(x_in)).then_inc(s_in_x, 16)
            for t, w in ((w_self_t, w_self), (w_neigh_t, w_neigh), (w_kvq_t, w_kvq), (w_edge_t, w_edge),
                         (w_gcn_t, w_gcn), (w_lr_t, w_lin_root)):
                sp.dma_start(t[:, :], w).then_inc(s_in_w, 16)
            sp.wait_ge(s_zeros, 1)
            for k in range(4):
                w = sums[k].shape[1]
                sp.dma_start(sums[k].rearrange("(p b) d -> p (b d)", p=P), zeros[:, 0:NB * w]).then_inc(s_zeroed, 16)
            npass = passes(sp)

            def load_idx(a, it, c, h):
                sp.wait_ge(a.used, it * CG + h * (CG // 2) + 1)
                sp.dma_start(idx[:, h, :], src_in[:, bass.ds(c * CT + h * HT, HT)]).then_inc(a.idx_ready[h], 16)

            def aggregate(k):
                a = L[k]
                with sp.Fori(0, npass) as p:
                    with sp.Fori(0, C) as c:
                        it = sp.snap(p * C + c)
                        for h in range(2):
                            load_idx(a, it, c, h)

            def attention():
                a = A
                with sp.Fori(0, npass) as p:
                    wait_alone(sp, a.pass_ready, p + 1)
                    with sp.Fori(0, C) as c:
                        it = sp.snap(p * C + c)
                        load_idx(a, it, c, 0)
                        b = sp.value_load(base_i[0:1, bass.ds(c + 1, 1)], min_val=0, max_val=LAST_BASE)
                        sp.wait_ge(a.qwin, it + 1)
                        sp.dma_start(q_land[:, :], q_tab[bass.ds(b, P), :]).then_inc(a.q_ready, 16)
                        for g in range(CG):
                            if g == CG // 2:
                                load_idx(a, it, c, 1)
                            sp.wait_ge(a.e_done, it * CG + g + 1)
                            sp.dma_start(ea[0:D, g % KV_RING, :],
                                         ea_in[:, bass.ds(c * (CT * P) + g * (G * P), G * P)]
                                         ).then_inc(a.ea_ready[g % KV_RING], 16)

            def load_sums(k, w):
                sp.wait_ge(sums_whole[k], 1)
                sp.dma_start(agg[:, :, 0:w], rows(sums[k])).then_inc(sums_loaded[k], 16)

            aggregate(0)
            load_sums(0, WA)
            sp.wait_ge(s_kvq, 1)
            sp.dma_start(rows(kv_tab), kvq[:, :, 0:2 * D]).then_inc(s_stored, 16)
            sp.dma_start(rows(q_tab), qs[:, :, :]).then_inc(s_stored, 16)
            sp.wait_ge(s_stored, 32)
            sp.sem_inc(L[1].go, 1)
            attention()
            load_sums(1, WT)
            sp.wait_ge(s_t2, 1)
            sp.dma_start(rows(t2_tab), ya[:, :, :]).then_inc(s_stored, 16)
            sp.wait_ge(s_stored, 48)
            sp.sem_inc(L[2].go, 1)
            aggregate(2)
            load_sums(2, WA)
            sp.wait_ge(s_t3, 1)
            sp.dma_start(rows(t3_tab), t3).then_inc(s_stored, 16)
            sp.wait_ge(s_stored, 64)
            sp.sem_inc(L[3].go, 1)
            aggregate(3)
            load_sums(3, WA)
            sp.wait_ge(s_final, 1)
            full = 3125 // P
            sp.dma_start(out[0:full * P, :].rearrange("(b p) d -> p b d", p=P), xa[:, 0:full, :]).then_inc(s_stored, 16)
            sp.dma_start(out[full * P:3125, :], xa[0:3125 - full * P, full, :]).then_inc(s_stored, 16)
            sp.wait_ge(s_stored, 96)

        @block.gpsimd
        def _(pool):
            nc.gpsimd.memset(ident[:, :], 0.0).then_inc(s_pool, 1)
            nc.gpsimd.iota(iota_i[:, :], [[1, P]], base=0, channel_multiplier=0).then_inc(s_pool, 1)
            pool.wait_ge(s_pool, 2)
            nc.gpsimd.affine_select(out=ident[:, :], in_=ident[:, :], compare_op=ALU.not_equal, fill=1.0, base=0,
                                    pattern=[[-1, P]], channel_multiplier=1).then_inc(s_ident, 1)
            npass = passes(pool)

            def add_window(a, k, w, b, n):
                pool.wait_ge(a.flush_ready, n + 1)
                pool.dma_start(sums[k][bass.ds(b, P), :], flush[:, 0:w], accum_op=ALU.add).then_inc(a.flushed, 16)

            def run(k, table, ring, w_row, w_sum):
                a = L[k]
                if k:
                    pool.wait_ge(a.go, 1)
                with pool.Fori(0, npass) as p:
                    wait_alone(pool, a.pass_ready, p + 1)
                    with pool.Fori(0, C) as c:
                        it = pool.snap(p * C + c)
                        for g in range(CG):
                            h = g // (CG // 2)
                            if g % (CG // 2) == 0:
                                pool.wait_ge(a.idx_ready[h], (it + 1) * 16)
                            wait_alone(pool, a.used, it * CG + g + 2)
                            for j in range(G):
                                col = (g % (CG // 2)) * G + j
                                pool.indirect_dma_start(
                                    ring[:, g % KV_RING, j, 0:w_row], None, table,
                                    bass.IndirectOffsetOnAxis(ap=idx[:, h, col:col + 1], axis=0)
                                    ).then_inc(a.gathered[g % KV_RING], 16)
                            if g == 2:
                                b = pool.value_load(base_i[0:1, bass.ds(c, 1)], min_val=0, max_val=LAST_BASE)
                                add_window(a, k, w_sum, b, p * (C + 1) + c)
                    b = pool.value_load(base_i[0:1, C:C + 1], min_val=0, max_val=LAST_BASE)
                    add_window(a, k, w_sum, b, p * (C + 1) + C)
                pool.wait_ge(a.flushed, npass * (16 * (C + 1)))
                nc.gpsimd.sem_inc(sums_whole[k], 1)

            pool.wait_ge(s_zeroed, 64)
            run(0, x_in, xg, D, WA)
            run(1, kv_tab, kv, 2 * D, WT)
            run(2, t2_tab, xg, D, WA)
            run(3, t3_tab, xg, D, WA)

        @block.scalar
        def _(act):
            npass = passes(act)

            def node(m, ins):
                act.wait_ge(n_go, m + 1)
                with act.Fori(0, NB // 2) as i:
                    for u in range(2):
                        n = i * 2 + (u + m * NB)
                        act.wait_ge(n_tr, n + 1)
                        for k, src in enumerate(ins):
                            last = nc.scalar.copy(xs[:, u, k * D:(k + 1) * D],
                                                  src[:, bass.ds(i * 2 + u, 1), 0:D].rearrange("p o d -> p (o d)"))
                        last.then_inc(n_staged, 1)
                    for u in range(2):
                        n = i * 2 + (u + m * NB)
                        act.wait_ge(n_tr, n + 3)
                        act.wait_ge(n_mm, n + 1)
                        w = len(ins) * P
                        nc.scalar.copy(xT[0:D, u, 0:w], N_t[u][0:D, 0:w]).then_inc(n_xT, 1)

            roots = [0]

            def root(ap):
                roots[0] += 1
                act.wait_ge(s_sqrt_in, roots[0])
                nc.scalar.activation(ap, ap, ACT.Sqrt).then_inc(s_sqrt, 1)

            root(dinv_in[:, :])
            node(0, [xa, za])
            root(stat[:, 2, :])
            node(1, [xa])
            a = A
            with act.Fori(0, npass) as p:
                with act.Fori(0, C) as c:
                    it = act.snap(p * C + c)
                    act.wait_ge(a.q_ready, (it + 1) * 16)
                    act.wait_ge(a.q_done, it * CG + 2)
                    nc.scalar.copy(q_win[:, :], q_land[:, :]).then_inc(a.qwin, 1)
                    for g in range(CG):
                        u, n = g % 2, it * CG + g
                        act.wait_ge(a.ohT_ps, n + 3)
                        act.wait_ge(a.q_done, n + 1)
                        nc.scalar.copy(ohT[:, u, :, :].rearrange("p g n -> p (g n)"), T_ps[u][:, 0:G * P]).then_inc(a.ohT_sb, 1)
                        act.wait_ge(a.seg, n + 1)
                        nc.scalar.copy(oh[:, u, :, :].rearrange("p g n -> p (g n)"),
                                       oh_b[:, u, :, :].rearrange("p g n -> p (g n)")).then_inc(a.oh32, 1)
                        act.wait_ge(a.sc, n + 1)
                        nc.scalar.activation(msg[:, u, :, D:WT], sc[:, u, :].rearrange("p (g h) -> p g h", h=H),
                                             ACT.Exp).then_inc(a.exp, 1)
            root(dinv_out[:, :])
            root(stat[:, 2, :])
            node(2, [za])
            root(stat[:, 2, :])
            node(3, [xa])
            root(stat[:, 2, :])

        @block.tensor
        def _(pe):
            pe.wait_ge(s_ident, 1)
            pe.wait_ge(s_prep, 4)
            for m in range(2):
                last = nc.tensor.transpose(bank[m][0:C, 0:P], cmin[:, m * C:(m + 1) * C], ident[:, :])
            last.then_inc(s_prep_pe, 1)
            pe.wait_ge(s_prep, 8)
            for m in range(2):
                last = nc.tensor.transpose(bank[2 + m][:, 0:C], cwide[:, m, :], ident[0:C, 0:C])
            last.then_inc(s_prep_pe, 1)

            zb = zeros[:, :].bitcast(bf16)
            pe.wait_ge(s_deg_oh, 1)
            nc.tensor.matmul(bank[7][:, 0:NB], zb[:, 0:P], zb[:, 0:NB], start=True, stop=False, skip_group_check=True)
            with pe.Fori(0, NT // (2 * G)) as i:
                for u in range(2):
                    pe.wait_ge(s_deg_oh, i * 2 + u + 2)
                    for j in range(G):
                        last = nc.tensor.matmul(bank[7][:, 0:NB], oh_b[:, u, j, :], oh_hi[:, u, j, :],
                                                start=False, stop=False, skip_group_check=True)
                    last.then_inc(s_deg_mm, 1)
            npass = passes(pe)

            def aggregate(k):
                a = L[k]
                with pe.Fori(0, npass) as p:
                    with pe.Fori(0, C) as c:
                        it = pe.snap(p * C + c)
                        pe.wait_ge(a.flush_ready, p * (C + 1) + c + 1)
                        for g in range(CG):
                            r = g % KV_RING
                            pe.wait_ge(a.gathered[r], (it * 2 + g // KV_RING + 1) * (16 * G))
                            pe.wait_ge(a.oh_ready, it * CG + g + 1)
                            for j in range(G):
                                last = nc.tensor.matmul(acc[:, 0:WA], oh[:, g % 2, j, :], xg[:, r, j, :],
                                                        start=(g == 0 and j == 0), stop=(g == CG - 1 and j == G - 1))
                            last.then_inc(a.used, 1)

            def node(m, widths, n_out):
                pe.wait_ge(n_go, m + 1)
                with pe.Fori(0, NB // 2) as i:
                    for u in range(2):
                        n = i * 2 + (u + m * NB)
                        pe.wait_ge(n_staged, n + 1)
                        pe.wait_ge(n_xT, n + 1)
                        for k in range(len(widths)):
                            last = nc.tensor.transpose(N_t[u][0:D, k * P:(k + 1) * P], xs[:, u, k * D:(k + 1) * D],
                                                       ident[:, :])
                        last.then_inc(n_tr, 1)
                    for u in range(2):
                        n = i * 2 + (u + m * NB)
                        pe.wait_ge(n_xT, n + 3)
                        pe.wait_ge(n_ev, n + 1)
                        for k, (w, w_rows) in enumerate(widths):
                            last = nc.tensor.matmul(N_o[u][:, 0:n_out], xT[0:w_rows, u, k * P:(k + 1) * P], w[:, :],
                                                    start=(k == 0), stop=(k == len(widths) - 1))
                        last.then_inc(n_mm, 1)

            aggregate(0)
            pe.wait_ge(s_in_w, 96)
            node(0, [(w_self_t, D + 1), (w_neigh_t, D)], D)
            node(1, [(w_kvq_t, D + 1)], 3 * D)

            a = A

            def segment(it, g):
                n = it * CG + g
                pe.wait_ge(a.used, n + USED0 + 1)
                pe.wait_ge(a.oh32, n + 3)
                for j in range(G):
                    last = nc.tensor.matmul(acc[:, 0:WT], oh[:, g % 2, j, :], msg[:, g % 2, j, :],
                                            start=(g == 0 and j == 0), stop=(g == CG - 1 and j == G - 1))
                last.then_inc(a.seg, 1)

            with pe.Fori(0, npass) as p:
                with pe.Fori(0, C) as c:
                    it = pe.snap(p * C + c)
                    for g in range(CG):
                        u, r, n = g % 2, g % KV_RING, it * CG + g
                        pe.wait_ge(a.ea_ready[r], (it * 2 + g // KV_RING + 1) * 16)
                        pe.wait_ge(a.t1, n + 1)
                        for j in range(G):
                            last = nc.tensor.matmul(E_ps[u][:, j * D:(j + 1) * D], ea[:, r, j * P:(j + 1) * P],
                                                    w_edge_t[:, :], start=True, stop=True)
                        last.then_inc(a.e_done, 1)
                        pe.wait_ge(a.oh_ready, n + 1)
                        pe.wait_ge(a.ohT_sb, n + 1)
                        for j in range(G):
                            last = nc.tensor.transpose(T_ps[u][:, j * P:(j + 1) * P], oh_b[:, u, j, :], ident_b[:, :])
                        last.then_inc(a.ohT_ps, 1)
                        if g == 0:
                            pe.wait_ge(a.flush_ready, p * (C + 1) + c + 1)
                            pe.wait_ge(a.qwin, it + 2)
                        else:
                            segment(it, g - 1)
                        pe.wait_ge(a.ohT_sb, n + 3)
                        pe.wait_ge(a.t2, n + 1)
                        for j in range(G):
                            for part in range(3):
                                last = nc.tensor.matmul(Q_ps[u][:, j * D:(j + 1) * D], ohT[:, u, j, :],
                                                        q_win[:, part * D:(part + 1) * D],
                                                        start=(part == 0), stop=(part == 2))
                        last.then_inc(a.q_done, 1)
                    segment(it, CG - 1)

            aggregate(2)
            node(2, [(w_gcn_t, D + 1)], D)
            node(3, [(w_lr_t, D + 1)], 2 * D)
            aggregate(3)

        @block.vector
        def _(dve):
            class Steps:
                def __init__(self, s, base=0):
                    self.s, self.n, self.base = s, 0, base

                def __call__(self, ins):
                    self.n += 1
                    ins.then_inc(self.s, 1)
                    dve.wait_ge(self.s, self.base + self.n)

            V = nc.vector
            V.memset(zeros[:, :], 0.0).then_inc(s_zeros, 1)
            for s_ in (n_tr, n_xT, n_mm, n_ev):
                V.sem_inc(s_, 2)
            for k in range(4):
                V.sem_inc(L[k].used, USED0)
            V.sem_inc(A.e_done, KV_RING)
            V.sem_inc(A.qwin, 1)
            for s_ in (A.oh32, A.ohT_ps, A.ohT_sb, A.q_done, A.t1, A.t2, A.seg):
                V.sem_inc(s_, 2)

            prep = Steps(s_prep)
            dve.wait_ge(s_in_e, 32)
            prep(V.tensor_copy(dst_f[:, :], dst_all[:, :]))
            prep(V.tensor_reduce(cmin[:, 0:C], dst_f[:, :].rearrange("p (c t) -> p c t", t=CT), AX, ALU.min))
            prep(V.scalar_tensor_tensor(out=slot0[:, :], in0=dst_f[:, :], scalar=float(PAD_DST), in1=dst_f[:, :],
                                        op0=ALU.is_lt, op1=ALU.mult))
            prep(V.tensor_reduce(cmin[:, C:2 * C], slot0[:, :].rearrange("p (c t) -> p c t", t=CT), AX, ALU.max))
            dve.wait_ge(s_prep_pe, 1)
            prep(V.tensor_reduce(cred[:, 0:1], bank[0][0:C, 0:P], AX, ALU.min))
            prep(V.tensor_reduce(cred[:, 1:2], bank[1][0:C, 0:P], AX, ALU.max))
            for m in range(2):
                prep(V.tensor_copy(cwide[:, m, :], cred[:, m:m + 1].broadcast_to([C, P])))
            dve.wait_ge(s_prep_pe, 2)
            prep(V.tensor_copy(base0[:, :], bank[2][:, 0:C]))
            prep(V.tensor_tensor(span_f[:, :], bank[3][0:1, 0:C], base0[0:1, :], ALU.subtract))
            prep(V.tensor_reduce(span_m[:, :], span_f[:, :], AX, ALU.max))
            prep(V.tensor_tensor(slot0[:, :].rearrange("p (c t) -> p c t", t=CT),
                                 dst_f[:, :].rearrange("p (c t) -> p c t", t=CT),
                                 base0[:, :].unsqueeze(2).broadcast_to([P, C, CT]), ALU.subtract))
            prep(V.memset(base_i[:, :], 0))
            V.tensor_copy(span_i[:, :], span_m[:, :]).then_inc(s_base, 1)
            dve.wait_ge(s_ident, 1)
            prep(V.tensor_copy(ident_b[:, :], ident[:, :]))
            prep(V.tensor_copy(iota_f[:, :], iota_i[:, :]))
            for t in (xT,):
                prep(V.memset(t[D:D + 1, :, :], 1.0))
            prep(V.memset(ea[D:D + 1, :, :], 1.0))
            prep(V.memset(xg[:, :, :, D:WA], 1.0))

            prep(V.tensor_scalar(lo_i[:, :], src_all[:, :], P - 1, None, ALU.bitwise_and))
            prep(V.tensor_scalar(hi_i[:, :], src_all[:, :], 7, None, ALU.logical_shift_right))
            prep(V.tensor_copy(lo_f[:, :], lo_i[:, :]))
            prep(V.tensor_copy(hi_f[:, :], hi_i[:, :]))
            prep(V.tensor_scalar(dst_f[:, :], dst_f[:, :], float(PAD_DST), float(PAD_DST), ALU.is_ge, ALU.mult))
            prep(V.tensor_tensor(hi_f[:, :], hi_f[:, :], dst_f[:, :], ALU.add))
            V.sem_inc(s_deg_oh, 1)
            V.sem_inc(s_deg_mm, 2)

            def onehot(dst, width, vals, at):
                return V.tensor_tensor(dst, iota_f[:, 0:width].unsqueeze(1).broadcast_to([P, G, width]),
                                       vals[:, bass.ds(at, G)].unsqueeze(2).broadcast_to([P, G, width]), ALU.is_equal)

            with dve.Fori(0, NT // (2 * G)) as i:
                for u in range(2):
                    dve.wait_ge(s_deg_mm, i * 2 + u + 1)
                    onehot(oh_b[:, u, :, :], P, lo_f, (i * 2 + u) * G)
                    onehot(oh_hi[:, u, :, :], NB, hi_f, (i * 2 + u) * G).then_inc(s_deg_oh, 1)
            dve.wait_ge(s_deg_mm, NT // G + 2)
            prep(V.tensor_scalar(outdeg[:, :], bank[7][:, 0:NB], 1.0, None, ALU.max))
            npass = passes(dve)

            def start_pass_state(k):
                a = L[k]
                st = Steps(a.step)
                st(V.tensor_copy(slot[:, :], slot0[:, :]))
                st(V.tensor_copy(base_f[:, :], base0[0:1, :]))
                return st

            def open_pass(k, p):
                a = L[k]
                st = Steps(a.step, p * 4 + 2)
                st(V.tensor_scalar(base_i[0:1, 1:C + 1], base_f[:, :], float(LAST_BASE), None, ALU.min))
                st(V.memset(flush[:, :], 0.0))
                V.sem_inc(a.pass_ready, 1)
                V.sem_inc(a.flush_ready, 1)

            def close_pass(k, p):
                dve.wait_ge(L[k].flushed, (p + 1) * (16 * (C + 1)))
                st = Steps(L[k].step, p * 4 + 4)
                st(V.tensor_scalar(slot[:, :], slot[:, :], float(-P), None, ALU.add))
                st(V.tensor_scalar(base_f[:, :], base_f[:, :], float(P), None, ALU.add))

            def copy_window(a, p, c, n, w):
                dve.wait_ge(a.flushed, (p * (C + 1) + c + 1) * 16)
                V.tensor_copy(flush[:, 0:w], acc[:, 0:w]).then_inc(a.flush_ready, 1)

            def aggregate(k):
                a = L[k]
                start_pass_state(k)
                with dve.Fori(0, npass) as p:
                    open_pass(k, p)
                    with dve.Fori(0, C) as c:
                        it = dve.snap(p * C + c)
                        for g in range(CG):
                            dve.wait_ge(a.used, it * CG + g + KV_RING)
                            onehot(oh[:, g % 2, :, :], P, slot, c * CT + g * G).then_inc(a.oh_ready, 1)
                        dve.wait_ge(a.used, (it + 1) * CG + USED0)
                        copy_window(a, p, c, it, WA)
                    close_pass(k, p)

            roots = [0]

            def root(ins):
                roots[0] += 1
                ins.then_inc(s_sqrt_in, 1)
                dve.wait_ge(s_sqrt, roots[0])

            def layer_norm(y, dst):
                wide = stat[:, 0, :].unsqueeze(2).broadcast_to([P, NB, D])
                st(V.tensor_reduce(stat[:, 0, :], y, AX, ALU.add))
                st(V.tensor_scalar(stat[:, 0, :], stat[:, 0, :], 1.0 / D, None, ALU.mult))
                st(V.tensor_tensor(y, y, wide, ALU.subtract))
                st(V.tensor_tensor(sq, y, y, ALU.mult))
                st(V.tensor_reduce(stat[:, 1, :], sq, AX, ALU.add))
                root(V.tensor_scalar(stat[:, 2, :], stat[:, 1, :], 1.0 / D, 1e-5, ALU.mult, ALU.add))
                st(V.reciprocal(stat[:, 3, :], stat[:, 2, :]))
                st(V.tensor_tensor(dst, y, stat[:, 3, :].unsqueeze(2).broadcast_to([P, NB, D]), ALU.mult))

            def node(m, n_out, evict):
                with dve.Fori(0, NB // 2) as i:
                    for u in range(2):
                        dve.wait_ge(n_mm, i * 2 + (u + m * NB + 3))
                        evict(i * 2 + u, N_o[u]).then_inc(n_ev, 1)
                dve.wait_ge(n_ev, (m + 1) * NB + 2)

            st = Steps(n_step)

            def blk(t, b, w=D):
                return t[:, bass.ds(b, 1), 0:w].rearrange("p o d -> p (o d)")

            aggregate(0)
            dve.wait_ge(sums_loaded[0], 16)
            st(V.tensor_scalar(indeg[:, :], agg[:, :, D:WA].rearrange("p b o -> p (b o)"), 1.0, None, ALU.max))
            root(V.tensor_copy(dinv_in[:, :], indeg[:, :]))
            st(V.reciprocal(dinv_in[:, :], dinv_in[:, :]))
            st(V.reciprocal(stat[:, 0, :], indeg[:, :]))
            dve.wait_ge(s_in_x, 16)
            V.tensor_tensor(za[:, :, :], agg[:, :, 0:D], stat[:, 0, :].unsqueeze(2).broadcast_to([P, NB, D]),
                            ALU.mult).then_inc(n_go, 1)
            node(0, D, lambda b, ps: V.tensor_tensor(blk(ya, b), blk(xa, b), ps[:, 0:D], ALU.add))
            layer_norm(ya[:, :, :], xa[:, :, :])
            V.sem_inc(n_go, 1)

            node(1, 3 * D, lambda b, ps: V.tensor_copy(blk(kvq, b, 3 * D), ps[:, 0:3 * D]))
            q = kvq[:, :, 2 * D:3 * D]
            st(V.tensor_scalar(q, q, QSCALE, None, ALU.mult))
            for part in range(3):
                piece = qs[:, :, part * D:(part + 1) * D]
                st(V.tensor_copy(piece, q))
                if part < 2:
                    st(V.tensor_tensor(q, q, piece, ALU.subtract))
            V.sem_inc(s_kvq, 1)

            a = A
            start_pass_state(1)

            def scores(it, g):
                u, r, n = g % 2, g % KV_RING, it * CG + g
                dve.wait_ge(a.e_done, n + KV_RING + 1)
                dve.wait_ge(a.gathered[r], (it * 2 + g // KV_RING + 1) * (16 * G))
                pr = prod[:, u, :].rearrange("p (g d) -> p g d", g=G)
                V.tensor_tensor(pr, kv[:, r, :, 0:D], E_ps[u][:, 0:G * D].rearrange("p (g d) -> p g d", g=G),
                                ALU.mult).then_inc(a.t1, 1)

            def reduce_scores(it, g):
                u, n = g % 2, it * CG + g
                dve.wait_ge(a.q_done, n + 3)
                dve.wait_ge(a.t1, n + 3)
                V.tensor_tensor(prod[:, u, :], prod[:, u, :], Q_ps[u][:, 0:G * D], ALU.mult).then_inc(a.t2, 1)
                dve.wait_ge(a.t2, n + 3)
                V.tensor_reduce(sc[:, u, :], prod[:, u, :].rearrange("p (s d) -> p s d", d=HD), AX,
                                ALU.add).then_inc(a.red, 1)
                dve.wait_ge(a.red, n + 1)
                V.tensor_scalar(sc[:, u, :], sc[:, u, :], -5.0, 5.0, ALU.max, ALU.min).then_inc(a.sc, 1)

            def messages(it, g):
                u, r, n = g % 2, g % KV_RING, it * CG + g
                dve.wait_ge(a.exp, n + 1)
                w = msg[:, u, :, D:WT].unsqueeze(3).broadcast_to([P, G, H, HD])
                V.tensor_tensor(msg[:, u, :, 0:D].rearrange("p g (h d) -> p g h d", h=H),
                                kv[:, r, :, D:2 * D].rearrange("p g (h d) -> p g h d", h=H), w,
                                ALU.mult).then_inc(a.used, 1)

            def slots(it, c, g):
                n = it * CG + g
                dve.wait_ge(a.ohT_ps, n + 1)
                dve.wait_ge(a.oh32, n + 1)
                onehot(oh_b[:, g % 2, :, :], P, slot, c * CT + g * G).then_inc(a.oh_ready, 1)

            with dve.Fori(0, npass) as p:
                open_pass(1, p)
                with dve.Fori(0, C) as c:
                    it = dve.snap(p * C + c)
                    slots(it, c, 0)
                    for g in range(CG):
                        scores(it, g)
                        if g:
                            messages(it, g - 1)
                        if g + 1 < CG:
                            slots(it, c, g + 1)
                        reduce_scores(it, g)
                    messages(it, CG - 1)
                    dve.wait_ge(a.seg, (it + 1) * CG + 2)
                    copy_window(a, p, c, it, WT)
                close_pass(1, p)

            dve.wait_ge(sums_loaded[1], 16)
            root(V.tensor_copy(dinv_out[:, :], outdeg[:, :]))
            st(V.reciprocal(dinv_out[:, :], dinv_out[:, :]))
            st(V.tensor_scalar(agg[:, :, D:WT], agg[:, :, D:WT], 1e-6, None, ALU.add))
            st(V.reciprocal(agg[:, :, D:WT], agg[:, :, D:WT]))
            for h in range(H):
                st(V.tensor_tensor(agg[:, :, h * HD:(h + 1) * HD], agg[:, :, h * HD:(h + 1) * HD],
                                   agg[:, :, D + h:D + h + 1].broadcast_to([P, NB, HD]), ALU.mult))
            st(V.tensor_tensor(ya[:, :, :], agg[:, :, 0:D], xa[:, :, :], ALU.add))
            layer_norm(ya[:, :, :], xa[:, :, :])
            V.tensor_tensor(ya[:, :, :], xa[:, :, :], dinv_out[:, :].unsqueeze(2).broadcast_to([P, NB, D]),
                            ALU.mult).then_inc(s_t2, 1)

            aggregate(2)
            dve.wait_ge(sums_loaded[2], 16)
            V.tensor_tensor(za[:, :, :], agg[:, :, 0:D], dinv_in[:, :].unsqueeze(2).broadcast_to([P, NB, D]),
                            ALU.mult).then_inc(n_go, 1)
            node(2, D, lambda b, ps: V.tensor_tensor(blk(ya, b), blk(xa, b), ps[:, 0:D], ALU.add))
            layer_norm(ya[:, :, :], xa[:, :, :])
            V.sem_inc(n_go, 1)

            node(3, 2 * D, lambda b, ps: V.tensor_copy(blk(kvq, b, 2 * D), ps[:, 0:2 * D]))
            V.tensor_tensor(t3, t3, dinv_in[:, :].unsqueeze(2).broadcast_to([P, NB, D]), ALU.mult).then_inc(s_t3, 1)
            aggregate(3)
            dve.wait_ge(sums_loaded[3], 16)
            st(V.tensor_tensor(ya[:, :, :], agg[:, :, 0:D], dinv_in[:, :].unsqueeze(2).broadcast_to([P, NB, D]), ALU.mult))
            st(V.tensor_tensor(ya[:, :, :], ya[:, :, :], r3, ALU.add))
            st(V.tensor_scalar(ya[:, :, :], ya[:, :, :], 0.0, None, ALU.max))
            st(V.tensor_tensor(ya[:, :, :], ya[:, :, :], xa[:, :, :], ALU.add))
            layer_norm(ya[:, :, :], xa[:, :, :])
            V.sem_inc(s_final, 1)


def kernel(x, src, dst, edge_attr_96, L0_gnn_W_self, L0_gnn_W_neigh, L0_gnn_b, L1_gnn_Wq, L1_gnn_bq, L1_gnn_Wk, L1_gnn_bk,
           L1_gnn_We, L1_gnn_be, L1_gnn_Wv, L1_gnn_bv, L2_gnn_weight, L2_gnn_bias, L3_gnn_W_lin, L3_gnn_b_lin,
           L3_gnn_W_root, L3_gnn_b_root):
    import numpy as np
    import concourse.bacc as bacc
    from concourse import mybir as mb
    from concourse.bass_utils import run_bass_kernel_spmd

    P, NR, NT, E, N = 128, 26 * 128, 810, 103125, 3125
    A = np.asarray

    def edges(a, fill):
        padded = np.full((NT * P,), fill, np.int32)
        padded[:E] = A(a)
        return np.ascontiguousarray(padded.reshape(NT, P).T)

    def with_bias(w, b):
        return np.ascontiguousarray(np.concatenate([A(w), A(b)[None, :]], axis=0))

    x_pad = np.zeros((NR, 96), np.float32)
    x_pad[:N] = A(x)
    ea_t = np.zeros((96, NT * P), np.float32)
    ea_t[:, :E] = A(edge_attr_96).T
    arrays = {
        "x_in": x_pad,
        "src_in": edges(src, 0),
        "dst_in": edges(dst, 1 << 20),
        "ea_in": ea_t,
        "w_self": with_bias(L0_gnn_W_self, L0_gnn_b),
        "w_neigh": np.ascontiguousarray(A(L0_gnn_W_neigh)),
        "w_kvq": np.concatenate([with_bias(L1_gnn_Wk, L1_gnn_bk), with_bias(L1_gnn_Wv, L1_gnn_bv),
                                 with_bias(L1_gnn_Wq, L1_gnn_bq)], axis=1),
        "w_edge": with_bias(L1_gnn_We, L1_gnn_be),
        "w_gcn": with_bias(L2_gnn_weight, L2_gnn_bias),
        "w_lin_root": np.concatenate([with_bias(A(L3_gnn_W_lin).T, L3_gnn_b_lin),
                                      with_bias(A(L3_gnn_W_root).T, L3_gnn_b_root)], axis=1),
    }
    nc = bacc.Bacc("TRN2", target_bir_lowering=False, num_devices=1)
    args = [nc.dram_tensor(n, list(a.shape), mb.dt.from_np(a.dtype), kind="ExternalInput").ap() for n, a in arrays.items()]
    out = nc.dram_tensor("out", [N, 96], mb.dt.float32, kind="ExternalOutput").ap()
    residual_gnn_kernel(nc, *args, out)
    r = run_bass_kernel_spmd(nc, [arrays], core_ids=[0])
    return r.results[0]["out"]
```

```python
import concourse.bass as bass
from concourse import mybir
from contextlib import ExitStack


def residual_gnn_kernel(nc, x_in, src_in, dst_in, ea_in, w_self, w_neigh, w_kvq, w_edge, w_gcn, w_lin_root, out, n_nodes, n_edges):
    fp32, bf16, i32 = mybir.dt.float32, mybir.dt.bfloat16, mybir.dt.int32
    fp16, u8 = mybir.dt.float16, mybir.dt.uint8
    ALU, ACT, AX = mybir.AluOpType, mybir.ActivationFunctionType, mybir.AxisListType.X

    P = 128
    D = 96
    H = 8
    HD = D // H
    NB = x_in.shape[0] // P
    NR = NB * P
    NT = src_in.shape[1]
    G = 5
    CG = 6
    CT = G * CG
    C = NT // CT
    HT = CT // 2
    KV_RING = 3
    USED0 = KV_RING + 1
    QSCALE = float(HD) ** -0.5
    PAD_DST = 1 << 20
    LAST_BASE = NR - P
    PASSES_MAX = (n_nodes - 1) // P + 1
    NH = (n_nodes + P - 1) // P
    SW = 16
    BT = 3
    BC = NT // BT
    KEYS = NH * SW
    ACT_H = 15

    ctx = ExitStack()
    with ctx:
        def sb(name, shape, dt=fp32):
            return ctx.enter_context(nc.sbuf_tensor(name, shape, dt))

        def pb(name, shape, dt=fp32):
            return ctx.enter_context(nc.psum_tensor(name, shape, dt))

        def sem(name):
            return ctx.enter_context(nc.semaphore(name))

        kv_tab = nc.dram_tensor("kv_tab", [NR, 2 * D], fp32, kind="Internal").ap()
        q_tab = nc.dram_tensor("q_tab", [NR, 3 * D], bf16, kind="Internal").ap()
        t2_tab = nc.dram_tensor("t2_tab", [NR, D], fp32, kind="Internal").ap()
        t3_tab = nc.dram_tensor("t3_tab", [NR, D], fp32, kind="Internal").ap()
        WA = D + 1
        WT = D + H
        sums = {0: nc.dram_tensor("sum0", [NR, WA], fp32, kind="Internal").ap(),
                1: nc.dram_tensor("sum1", [NR, WT], fp32, kind="Internal").ap(),
                2: nc.dram_tensor("sum2", [NR, WA], fp32, kind="Internal").ap(),
                3: nc.dram_tensor("sum3", [NR, WA], fp32, kind="Internal").ap()}
        tables = {0: x_in, 2: t2_tab, 3: t3_tab}

        def rows(ap):
            return ap.rearrange("(b p) d -> p b d", p=P)

        ident = sb("ident", [P, P])
        ident_b = sb("ident_b", [P, P], bf16)
        iota_i = sb("iota_i", [P, P], i32)
        iota_f = sb("iota_f", [P, P])
        key_i = sb("key_i", [P, KEYS], i32)
        iota_h = sb("iota_h", [P, KEYS], fp16)
        ones = sb("ones", [P, P])
        iota_6 = sb("iota_6", [P, P, 2 * BT], bf16)
        lo_h = sb("lo_h", [P, NT], bf16)
        zero_b = sb("zero_b", [P, P], bf16)
        first_f = sb("first_f", [1, BC])
        first_i = sb("first_i", [1, BC + 2], i32)
        degsum = sb("degsum", [P, 1])
        bad_f = sb("bad_f", [1, 1])
        bad_i = sb("bad_i", [1, 1], i32)
        carry = sb("carry", [P, BC])
        carry_h = sb("carry_h", [P, BC], bf16)
        iota_c = sb("iota_c", [P, NH, 1], bf16)
        outpart = sb("outpart", [P, NH])
        src_all = sb("src_all", [P, NT], i32)
        dst_all = sb("dst_all", [P, NT], i32)
        dst_f = sb("dst_f", [P, NT])
        slot0 = sb("slot0", [P, NT])
        slot = sb("slot", [P, NT])
        key = slot
        cmin = sb("cmin", [P, 2 * C])
        cred = sb("cred", [C, 2])
        cwide = sb("cwide", [C, 2, P])
        base0 = sb("base0", [P, C])
        base_f = sb("base_f", [1, C])
        base_i = sb("base_i", [1, C + 1], i32)
        span_f = sb("span_f", [1, C])
        span_m = sb("span_m", [1, 1])
        span_i = sb("span_i", [1, 1], i32)

        xa = sb("xa", [P, NB, D])
        ya = sb("ya", [P, NB, D])
        agg = sb("agg", [P, NB, WT])
        sq = agg[:, :, 0:D]
        stat = sb("stat", [P, 4, NB])
        outdeg = sb("outdeg", [P, NB])
        indeg = sb("indeg", [P, NB])
        dinv_out = sb("dinv_out", [P, NB])
        dinv_in = sb("dinv_in", [P, NB])
        parts = sb("parts", [P, NB, 3 * D + 2], bf16)
        MID, LOW, HIGH, ONE = 0, D, 2 * D, 3 * D
        counts = sb("counts", [P, NH, NH * P], u8)

        area = sb("area", [P, NB * 3 * D])
        kvq = area[:, :].rearrange("p (b d) -> p b d", d=3 * D)
        at = 0

        def carve(n):
            nonlocal at
            at += n
            return area[:, at - n:at]

        kv = carve(KV_RING * G * 2 * D).rearrange("p (r g d) -> p r g d", r=KV_RING, g=G)
        oh = carve(2 * G * P).rearrange("p (u g n) -> p u g n", u=2, g=G)
        ea = carve(KV_RING * G * P).rearrange("p (r n) -> p r n", r=KV_RING)
        prod = carve(2 * G * D).rearrange("p (u n) -> p u n", u=2)
        r3 = area[:, (KV_RING * 2 * D + 2 * P) * G:][:, 0:NB * D].rearrange("p (b d) -> p b d", d=D)
        block_b = area[:, 0:NH * P].bitcast(bf16).rearrange("p (u h n) -> p u h n", u=2, h=NH)
        BR = 4
        key_oh = area[:, 0:BR * BT * KEYS // 2].bitcast(bf16).rearrange("p (u t n) -> p u t n", u=BR, t=BT)
        lo_oh = area[:, BR * BT * KEYS // 2:][:, 0:BR * BT * P].bitcast(bf16).rearrange("p (u n t) -> p u n t", u=BR, n=P)
        carry_oh = area[:, BR * BT * (KEYS // 2 + P):][:, 0:NH * BC // 2].bitcast(bf16).rearrange("p (h c) -> p h c", h=NH)

        w_self_t = sb("w_self_t", [D + 1, D])
        w_neigh_t = sb("w_neigh_t", [D, D])
        w_kvq_t = sb("w_kvq_t", [D + 1, 3 * D])
        w_edge_t = sb("w_edge_t", [D + 1, D])
        w_gcn_t = sb("w_gcn_t", [D + 1, D])
        w_lr_t = sb("w_lr_t", [D + 1, 2 * D])

        xs = sb("xs", [P, 2, 2 * D])
        xT = sb("xT", [D + 1, 2, 2 * P])

        idx = sb("idx", [P, 2, HT], i32)
        oh_b = sb("oh_b", [P, 2, G, P], bf16)
        ohT = sb("ohT", [P, 2, G, P], bf16)
        q_land = sb("q_land", [P, 3 * D], bf16)
        q_win = sb("q_win", [P, 3 * D], bf16)
        sc = sb("sc", [P, 2, G * H])
        msg = sb("msg", [P, 2, G, WT])
        flush = sb("flush", [P, WT])

        lo_f = sb("lo_f", [P, NT])
        oh_hi = sb("oh_hi", [P, 2, G, NB], bf16)

        bank = [pb(f"bank{i}", [P, 512]) for i in range(8)]
        E_ps = [bank[0], bank[1]]
        Q_ps = [bank[2], bank[3]]
        T_ps = [bank[4][:, :].bitcast(bf16), bank[5][:, :].bitcast(bf16)]
        acc = bank[6]
        N_t = [bank[0], bank[1]]
        N_o = [bank[2], bank[3]]

        s_in_x, s_in_e, s_in_w, s_zeroed = sem("in_x"), sem("in_e"), sem("in_w"), sem("zeroed")
        s_zeros = sem("zeros_ready")
        s_pool = sem("pool_step")
        s_ident = sem("ident_ready")
        s_identb = sem("identb_ready")
        s_prep = sem("prep_step")
        s_prep_pe = sem("prep_transposed")
        s_base = sem("bases_ready")
        s_deg_oh, s_deg_mm = sem("deg_onehot"), sem("deg_summed")
        b_clear, b_oh, b_mm, b_wr = (sem("counts_clear"), sem("window_onehot"), sem("window_summed"),
                                            sem("window_written"))
        d_go, d_cv, d_ca, d_mm, d_ea, d_st, d_ev = (sem("dense_parts"), sem("dense_block_dve"), sem("dense_block_act"),
                                              sem("dense_product"), sem("dense_high_part"), sem("dense_mid_part"), sem("dense_evicted"))
        s_degsum, s_total, s_bad = sem("degree_sums"), sem("total"), sem("bad_known")
        s_outdeg = sem("outdeg_step")
        d_parts = sem("dense_dve_step")
        deg_step = sem("outdeg_dve_step")
        s_tab2, s_tab3 = sem("t2_stored"), sem("t3_stored")

        block = ctx.enter_context(nc.Block())

        class Agg:
            def __init__(self, k):
                n = f"L{k}_"
                self.idx_ready = [sem(n + f"idx_ready{i}") for i in range(2)]
                self.gathered = [sem(n + f"gathered{i}") for i in range(KV_RING)]
                self.used = sem(n + "used")
                self.oh_ready = sem(n + "onehot")
                self.chunk_summed = sem(n + "chunk_summed")
                self.flush_ready = sem(n + "flush_ready")
                self.flushed = sem(n + "flushed")
                self.pass_ready = sem(n + "pass_ready")
                self.go = sem(n + "table_ready")
                self.step = sem(n + "dve_step")

        L = {k: Agg(k) for k in range(4)}
        A = L[1]
        A.q_ready, A.qwin = sem("L1_q_loaded"), sem("L1_q_window")
        A.ea_ready = [sem(f"L1_ea_ready{i}") for i in range(KV_RING)]
        A.e_done, A.ohT_ps, A.ohT_sb, A.q_done = sem("L1_e"), sem("L1_ohT_ps"), sem("L1_ohT_sb"), sem("L1_q")
        A.oh32, A.t1, A.t2, A.red, A.sc, A.exp, A.seg = (sem("L1_oh32"), sem("L1_t1"), sem("L1_t2"), sem("L1_red"),
                                                         sem("L1_scores"), sem("L1_exp"), sem("L1_segment"))

        n_go, n_staged, n_tr, n_xT = sem("node_input"), sem("node_staged"), sem("node_transposed"), sem("node_xT")
        n_mm, n_ev, n_step = sem("node_product"), sem("node_evicted"), sem("node_dve_step")
        s_sqrt_in, s_sqrt = sem("sqrt_input"), sem("sqrt_done")
        s_kvq, s_t2, s_t3, s_final = sem("kvq_ready"), sem("t2_ready"), sem("t3_ready"), sem("final_ready")
        s_stored = sem("stored")
        s_waited = sem("waited")
        sums_whole = [sem(f"sums{k}_whole") for k in range(4)]
        sums_loaded = [sem(f"sums{k}_loaded") for k in range(4)]

        def passes(eng):
            eng.wait_ge(s_base, 1)
            span = eng.value_load(span_i[0:1, 0:1], min_val=0, max_val=n_nodes - 1)
            return eng.snap(span // P + 1, min_val=1, max_val=PASSES_MAX)

        def load_bad(eng):
            eng.wait_ge(s_bad, 1)
            return eng.value_load(bad_i[0:1, 0:1], min_val=0, max_val=1)

        def load_firsts(eng, c):
            return nc.values_load_multi_w_load_instructions(first_i[0:1, bass.ds(c, BR)], engines=[eng.engine],
                                                            min_val=0, max_val=n_nodes)[1]

        def wait_alone(eng, s, value):
            eng.wait_ge(s, value)
            eng.sem_inc(s_waited, 1)

        @block.sync
        def _(sp):
            sp.dma_start(dst_all[:, :], dst_in).then_inc(s_in_e, 16)
            sp.dma_start(src_all[:, :], src_in).then_inc(s_in_e, 16)
            sp.dma_start(xa[:, :, :], rows(x_in)).then_inc(s_in_x, 16)
            for t, w in ((w_self_t, w_self), (w_neigh_t, w_neigh), (w_kvq_t, w_kvq), (w_edge_t, w_edge),
                         (w_gcn_t, w_gcn), (w_lr_t, w_lin_root)):
                sp.dma_start(t[:, :], w).then_inc(s_in_w, 16)
            sp.wait_ge(s_zeros, 1)
            for k in range(4):
                w = sums[k].shape[1]
                sp.dma_start(sums[k].rearrange("(p b) d -> p (b d)", p=P),
                             agg[:, :, :].rearrange("p b d -> p (b d)")[:, 0:NB * w]).then_inc(s_zeroed, 16)
            npass = passes(sp)

            def load_idx(a, it, c, h):
                sp.wait_ge(a.used, it * CG + h * (CG // 2) + 1)
                sp.dma_start(idx[:, h, :], src_in[:, bass.ds(c * CT + h * HT, HT)]).then_inc(a.idx_ready[h], 16)

            def aggregate(k):
                a = L[k]
                with sp.Fori(0, npass) as p:
                    with sp.Fori(0, C) as c:
                        it = sp.snap(p * C + c)
                        for h in range(2):
                            load_idx(a, it, c, h)

            def attention():
                a = A
                sp.wait_ge(a.go, 2)
                with sp.Fori(0, npass) as p:
                    wait_alone(sp, a.pass_ready, p + 1)
                    with sp.Fori(0, C) as c:
                        it = sp.snap(p * C + c)
                        load_idx(a, it, c, 0)
                        b = sp.value_load(base_i[0:1, bass.ds(c + 1, 1)], min_val=0, max_val=LAST_BASE)
                        sp.wait_ge(a.qwin, it + 1)
                        sp.dma_start(q_land[:, :], q_tab[bass.ds(b, P), :]).then_inc(a.q_ready, 16)
                        for g in range(CG):
                            if g == CG // 2:
                                load_idx(a, it, c, 1)
                            sp.wait_ge(a.e_done, it * CG + g + 1)
                            sp.dma_start(ea[0:D, g % KV_RING, :],
                                         ea_in[:, bass.ds(c * (CT * P) + g * (G * P), G * P)]
                                         ).then_inc(a.ea_ready[g % KV_RING], 16)

            def load_sums(k, w):
                sp.wait_ge(sums_whole[k], 1)
                sp.dma_start(agg[:, :, 0:w], rows(sums[k])).then_inc(sums_loaded[k], 16)

            bad = load_bad(sp)
            with sp.If(bad):
                aggregate(0)
                load_sums(0, WA)
            sp.wait_ge(s_kvq, 1)
            sp.dma_start(rows(kv_tab), kvq[:, :, 0:2 * D]).then_inc(s_stored, 16)
            sp.dma_start(rows(q_tab), parts[:, :, 0:3 * D]).then_inc(s_stored, 16)
            sp.wait_ge(s_stored, 32)
            sp.sem_inc(L[1].go, 1)
            attention()
            load_sums(1, WT)
            with sp.If(bad):
                sp.wait_ge(s_t2, 1)
                sp.dma_start(rows(t2_tab), ya[:, :, :]).then_inc(s_tab2, 16)
                sp.wait_ge(s_tab2, 16)
                sp.sem_inc(L[2].go, 1)
                aggregate(2)
                load_sums(2, WA)
            with sp.If(bad):
                sp.wait_ge(s_t3, 1)
                sp.dma_start(rows(t3_tab), ya[:, :, :]).then_inc(s_tab3, 16)
                sp.wait_ge(s_tab3, 16)
                sp.sem_inc(L[3].go, 1)
                aggregate(3)
                load_sums(3, WA)
            sp.wait_ge(s_final, 1)
            full = n_nodes // P
            sp.dma_start(out[0:full * P, :].rearrange("(b p) d -> p b d", p=P), xa[:, 0:full, :]).then_inc(s_stored, 16)
            sp.dma_start(out[full * P:n_nodes, :], xa[0:n_nodes - full * P, full, :]).then_inc(s_stored, 16)
            sp.wait_ge(s_stored, 64)

        @block.gpsimd
        def _(pool):
            nc.gpsimd.memset(ident[:, :], 0.0).then_inc(s_pool, 1)
            nc.gpsimd.iota(iota_i[:, :], [[1, P]], base=0, channel_multiplier=0).then_inc(s_pool, 1)
            nc.gpsimd.iota(key_i[:, :], [[1, KEYS]], base=0, channel_multiplier=0).then_inc(s_pool, 1)
            pool.wait_ge(s_pool, 1)
            nc.gpsimd.affine_select(out=ident[:, :], in_=ident[:, :], compare_op=ALU.not_equal, fill=1.0, base=0,
                                    pattern=[[-1, P]], channel_multiplier=1).then_inc(s_ident, 1)
            nc.gpsimd.memset(counts[:, :, :].rearrange("p h n -> p (h n)").bitcast(i32), 0).then_inc(b_clear, 1)
            npass = passes(pool)

            def add_window(a, k, w, b, n):
                pool.wait_ge(a.flush_ready, n + 1)
                pool.dma_start(sums[k][bass.ds(b, P), :], flush[:, 0:w], accum_op=ALU.add).then_inc(a.flushed, 16)

            def run(k, table, w_row, w_sum):
                a = L[k]
                pool.wait_ge(a.go, 2 if k else 1)
                with pool.Fori(0, npass) as p:
                    wait_alone(pool, a.pass_ready, p + 1)
                    with pool.Fori(0, C) as c:
                        it = pool.snap(p * C + c)
                        for g in range(CG):
                            h = g // (CG // 2)
                            if g % (CG // 2) == 0:
                                pool.wait_ge(a.idx_ready[h], (it + 1) * 16)
                            wait_alone(pool, a.used, it * CG + g + 2)
                            for j in range(G):
                                col = (g % (CG // 2)) * G + j
                                pool.indirect_dma_start(
                                    kv[:, g % KV_RING, j, 0:w_row], None, table,
                                    bass.IndirectOffsetOnAxis(ap=idx[:, h, col:col + 1], axis=0)
                                    ).then_inc(a.gathered[g % KV_RING], 16)
                            if g == 4:
                                b = pool.value_load(base_i[0:1, bass.ds(c, 1)], min_val=0, max_val=LAST_BASE)
                                add_window(a, k, w_sum, b, p * (C + 1) + c)
                    b = pool.value_load(base_i[0:1, C:C + 1], min_val=0, max_val=LAST_BASE)
                    add_window(a, k, w_sum, b, p * (C + 1) + C)
                pool.wait_ge(a.flushed, npass * (16 * (C + 1)))
                nc.gpsimd.sem_inc(sums_whole[k], 1)

            pool.wait_ge(s_zeroed, 64)
            bad = load_bad(pool)
            with pool.If(bad):
                run(0, x_in, D, WA)
            run(1, kv_tab, 2 * D, WT)
            with pool.If(bad):
                run(2, t2_tab, D, WA)
            with pool.If(bad):
                run(3, t3_tab, D, WA)

        @block.scalar
        def _(act):
            nc.scalar.preload_act_table(ACT.Sqrt)
            act.wait_ge(b_clear, 1)
            act.wait_ge(b_oh, 1)
            def write_window(c, u, first):
                    act.wait_ge(b_mm, c + BR + 1)
                    act.wait_ge(b_wr, c + BR)
                    nc.scalar.copy(counts[:, :, bass.ds(first, SW)],
                                   bank[u][:, 0:KEYS].rearrange("p (h n) -> p h n", n=SW)).then_inc(b_wr, 1)

            with act.Fori(0, BC // BR) as i:
                firsts = load_firsts(act, i * BR)
                for w in range(BR):
                    write_window(i * BR + w, w, firsts[w])
            firsts = load_firsts(act, BC // BR * BR)
            for w in range(BC % BR):
                write_window(BC // BR * BR + w, w, firsts[w])

            def dense(m):
                def convert(b, u):
                    act.wait_ge(d_mm, b + (m * NH + 1))
                    nc.scalar.copy(block_b[:, u, 0:ACT_H, :], counts[:, 0:ACT_H, bass.ds(b * P, P)]).then_inc(d_ca, 1)

                def evict(b, u):
                    act.wait_ge(d_mm, b + (m * NH + 3))
                    nc.scalar.copy(agg[:, bass.ds(b, 1), 0:WA].rearrange("p o d -> p (o d)"),
                                   N_o[u][:, HIGH:HIGH + WA]).then_inc(d_ea, 1)

                act.wait_ge(d_go, m + 1)
                convert(0, 0)
                with act.Fori(0, NH // 2) as i:
                    for u in range(2):
                        convert(i * 2 + (u + 1), 1 - u)
                        evict(i * 2 + u, u)
                evict(NH - 1, 0)

            npass = passes(act)

            def node(m, ins):
                act.wait_ge(n_go, m + 1)
                with act.Fori(0, NB // 2) as i:
                    for u in range(2):
                        n = i * 2 + (u + m * NB)
                        act.wait_ge(n_tr, n + 1)
                        for k, src in enumerate(ins):
                            last = nc.scalar.copy(xs[:, u, k * D:(k + 1) * D],
                                                  src[:, bass.ds(i * 2 + u, 1), 0:D].rearrange("p o d -> p (o d)"))
                        last.then_inc(n_staged, 1)
                    for u in range(2):
                        n = i * 2 + (u + m * NB)
                        act.wait_ge(n_tr, n + 3)
                        act.wait_ge(n_mm, n + 1)
                        w = len(ins) * P
                        nc.scalar.copy(xT[0:D, u, 0:w], N_t[u][0:D, 0:w]).then_inc(n_xT, 1)

            roots = [0]

            def root(ap):
                roots[0] += 1
                act.wait_ge(s_sqrt_in, roots[0])
                nc.scalar.activation(ap, ap, ACT.Sqrt).then_inc(s_sqrt, 1)

            dense(0)
            bad = load_bad(act)
            root(dinv_in[:, :])
            node(0, [xa, agg])
            root(stat[:, 2, :])
            node(1, [xa])
            a = A
            nc.scalar.preload_act_table(ACT.Exp)
            with act.Fori(0, npass) as p:
                with act.Fori(0, C) as c:
                    it = act.snap(p * C + c)
                    act.wait_ge(a.q_ready, (it + 1) * 16)
                    act.wait_ge(a.q_done, it * CG + 2)
                    nc.scalar.copy(q_win[:, :], q_land[:, :]).then_inc(a.qwin, 1)
                    for g in range(CG):
                        u, n = g % 2, it * CG + g
                        act.wait_ge(a.ohT_ps, n + 3)
                        act.wait_ge(a.q_done, n + 1)
                        nc.scalar.copy(ohT[:, u, :, :].rearrange("p g n -> p (g n)"), T_ps[u][:, 0:G * P]).then_inc(a.ohT_sb, 1)
                        act.wait_ge(a.seg, n + 1)
                        nc.scalar.copy(oh[:, u, :, :].rearrange("p g n -> p (g n)"),
                                       oh_b[:, u, :, :].rearrange("p g n -> p (g n)")).then_inc(a.oh32, 1)
                        act.wait_ge(a.sc, n + 1)
                        nc.scalar.activation(msg[:, u, :, D:WT], sc[:, u, :].rearrange("p (g h) -> p g h", h=H),
                                             ACT.Exp).then_inc(a.exp, 1)
                    act.wait_ge(a.seg, (it + 1) * CG + 2)
                    act.wait_ge(a.flushed, (p * (C + 1) + c + 1) * 16)
                    nc.scalar.copy(flush[:, 0:WT], acc[:, 0:WT]).then_inc(a.flush_ready, 1)
            root(dinv_out[:, :])
            root(stat[:, 2, :])
            with act.If(bad):
                act.nop()
            with act.Else():
                dense(1)
            node(2, [agg])
            root(stat[:, 2, :])
            node(3, [xa])
            with act.If(bad):
                act.nop()
            with act.Else():
                dense(2)
            root(stat[:, 2, :])

        @block.tensor
        def _(pe):
            pe.wait_ge(s_ident, 1)
            pe.wait_ge(s_prep, 4)
            for m in range(2):
                last = nc.tensor.transpose(bank[m][0:C, 0:P], cmin[:, m * C:(m + 1) * C], ident[:, :])
            last.then_inc(s_prep_pe, 1)
            pe.wait_ge(s_prep, 8)
            for m in range(2):
                last = nc.tensor.transpose(bank[2 + m][:, 0:C], cwide[:, m, :], ident[0:C, 0:C])
            last.then_inc(s_prep_pe, 1)

            pe.wait_ge(s_prep, 15)
            nc.tensor.matmul(bank[4][:, 0:BC], ones[0:1, :], first_f[0:1, :], start=True, stop=True).then_inc(s_prep_pe, 1)
            def window(c, w):
                bank_w = bank[w % BR][:, 0:KEYS]
                pe.wait_ge(b_oh, c + 1)
                pe.wait_ge(b_wr, c + 1)
                for t in range(BT):
                    nc.tensor.matmul(bank_w, lo_oh[:, w // 2, :, (w % 2) * BT + t], key_oh[:, w % BR, t, :],
                                     start=(t == 0), stop=False, skip_group_check=True)
                before = (w - 1) % (2 * BR)
                nc.tensor.matmul(bank_w.rearrange("p (h n) -> p h n", n=SW)[:, :, 0],
                                 lo_oh[:, before // 2, :, (before % 2) * BT + BT - 1],
                                 carry_oh[:, :, bass.ds(c, 1)].rearrange("p h o -> p (h o)"),
                                 start=False, stop=True, skip_group_check=True).then_inc(b_mm, 1)

            with pe.Fori(0, BC // (2 * BR)) as i:
                for w in range(2 * BR):
                    window(i * (2 * BR) + w, w)
            for w in range(BC % (2 * BR)):
                window(BC // (2 * BR) * (2 * BR) + w, w)

            def dense(m):
                def product(b, u):
                    n = b + m * NH
                    pe.wait_ge(d_ca, n + 1)
                    pe.wait_ge(d_cv, n + 1)
                    pe.wait_ge(d_ev, n + 1)
                    for h in range(NH):
                        last = nc.tensor.matmul(N_o[u][:, 0:ONE + 1], block_b[:, u, h, :], parts[:, h, 0:ONE + 1],
                                                start=(h == 0), stop=(h == NH - 1))
                    last.then_inc(d_mm, 1)

                with pe.Fori(0, NH // 2) as i:
                    for u in range(2):
                        product(i * 2 + u, u)
                product(NH - 1, 0)

            def out_degrees():
                pe.wait_ge(s_deg_oh, 1)
                nc.tensor.matmul(bank[7][:, 0:NB], zero_b[:, :], zero_b[:, 0:NB], start=True, stop=False,
                                 skip_group_check=True)
                with pe.Fori(0, NT // (2 * G)) as i:
                    for u in range(2):
                        pe.wait_ge(s_deg_oh, i * 2 + u + 2)
                        for j in range(G):
                            last = nc.tensor.matmul(bank[7][:, 0:NB], oh_b[:, u, j, :], oh_hi[:, u, j, :],
                                                    start=False, stop=False, skip_group_check=True)
                        last.then_inc(s_deg_mm, 1)

            npass = passes(pe)

            def aggregate(k):
                a = L[k]
                with pe.Fori(0, npass) as p:
                    with pe.Fori(0, C) as c:
                        it = pe.snap(p * C + c)
                        pe.wait_ge(a.flush_ready, p * (C + 1) + c + 1)
                        for g in range(CG):
                            r = g % KV_RING
                            pe.wait_ge(a.gathered[r], (it * 2 + g // KV_RING + 1) * (16 * G))
                            pe.wait_ge(a.oh_ready, it * CG + g + 1)
                            for j in range(G):
                                last = nc.tensor.matmul(acc[:, 0:WA], oh[:, g % 2, j, :], kv[:, r, j, 0:WA],
                                                        start=(g == 0 and j == 0), stop=(g == CG - 1 and j == G - 1))
                            last.then_inc(a.used, 1)

            def node(m, widths, n_out):
                pe.wait_ge(n_go, m + 1)
                with pe.Fori(0, NB // 2) as i:
                    for u in range(2):
                        n = i * 2 + (u + m * NB)
                        pe.wait_ge(n_staged, n + 1)
                        pe.wait_ge(n_xT, n + 1)
                        for k in range(len(widths)):
                            last = nc.tensor.transpose(N_t[u][0:D, k * P:(k + 1) * P], xs[:, u, k * D:(k + 1) * D],
                                                       ident[:, :])
                        last.then_inc(n_tr, 1)
                    for u in range(2):
                        n = i * 2 + (u + m * NB)
                        pe.wait_ge(n_xT, n + 3)
                        pe.wait_ge(n_ev, n + 1)
                        for k, (w, w_rows) in enumerate(widths):
                            last = nc.tensor.matmul(N_o[u][:, 0:n_out], xT[0:w_rows, u, k * P:(k + 1) * P], w[:, :],
                                                    start=(k == 0), stop=(k == len(widths) - 1))
                        last.then_inc(n_mm, 1)

            dense(0)
            pe.wait_ge(s_degsum, 1)
            nc.tensor.matmul(bank[4][0:1, 0:1], degsum[:, :], ones[:, 0:1], start=True, stop=True).then_inc(s_total, 1)
            bad = load_bad(pe)
            with pe.If(bad):
                aggregate(0)
            pe.wait_ge(s_in_w, 96)
            node(0, [(w_self_t, D + 1), (w_neigh_t, D)], D)
            node(1, [(w_kvq_t, D + 1)], 3 * D)

            a = A

            def segment(it, g):
                n = it * CG + g
                pe.wait_ge(a.used, n + USED0 + 1)
                pe.wait_ge(a.oh32, n + 3)
                for j in range(G):
                    last = nc.tensor.matmul(acc[:, 0:WT], oh[:, g % 2, j, :], msg[:, g % 2, j, :],
                                            start=(g == 0 and j == 0), stop=(g == CG - 1 and j == G - 1))
                last.then_inc(a.seg, 1)

            with pe.Fori(0, npass) as p:
                with pe.Fori(0, C) as c:
                    it = pe.snap(p * C + c)
                    for g in range(CG):
                        u, r, n = g % 2, g % KV_RING, it * CG + g
                        pe.wait_ge(a.oh_ready, n + 1)
                        pe.wait_ge(a.ohT_sb, n + 1)
                        for j in range(G):
                            last = nc.tensor.transpose(T_ps[u][:, j * P:(j + 1) * P], oh_b[:, u, j, :], ident_b[:, :])
                        last.then_inc(a.ohT_ps, 1)
                        pe.wait_ge(a.ea_ready[r], (it * 2 + g // KV_RING + 1) * 16)
                        pe.wait_ge(a.t1, n + 1)
                        for j in range(G):
                            last = nc.tensor.matmul(E_ps[u][:, j * D:(j + 1) * D], ea[0:D + 1, r, j * P:(j + 1) * P],
                                                    w_edge_t[:, :], start=True, stop=True)
                        last.then_inc(a.e_done, 1)
                        if g == 0:
                            pe.wait_ge(a.qwin, it + 2)
                        pe.wait_ge(a.ohT_sb, n + 3)
                        pe.wait_ge(a.t2, n + 1)
                        for j in range(G):
                            for part in range(3):
                                last = nc.tensor.matmul(Q_ps[u][:, j * D:(j + 1) * D], ohT[:, u, j, :],
                                                        q_win[:, part * D:(part + 1) * D],
                                                        start=(part == 0), stop=(part == 2))
                        last.then_inc(a.q_done, 1)
                        if g:
                            segment(it, g - 1)
                        else:
                            pe.wait_ge(a.flush_ready, p * (C + 1) + c + 1)
                    segment(it, CG - 1)

            with pe.If(bad):
                out_degrees()
            with pe.If(bad):
                aggregate(2)
            with pe.Else():
                dense(1)
            node(2, [(w_gcn_t, D + 1)], D)
            node(3, [(w_lr_t, D + 1)], 2 * D)
            with pe.If(bad):
                aggregate(3)
            with pe.Else():
                dense(2)

        @block.vector
        def _(dve):
            class Steps:
                def __init__(self, s, base=0):
                    self.s, self.n, self.base = s, 0, base

                def __call__(self, ins):
                    self.n += 1
                    ins.then_inc(self.s, 1)
                    dve.wait_ge(self.s, self.base + self.n)

            V = nc.vector
            V.memset(agg[:, :, :], 0.0).then_inc(s_zeros, 1)
            for s_ in (n_tr, n_xT, n_mm, n_ev):
                V.sem_inc(s_, 2)
            for k in range(4):
                V.sem_inc(L[k].used, USED0)
            V.sem_inc(A.e_done, KV_RING)
            V.sem_inc(A.qwin, 1)
            V.sem_inc(b_wr, BR)
            V.sem_inc(b_mm, BR)
            for s_ in (d_mm, d_ev):
                V.sem_inc(s_, 2)
            for s_ in (A.oh32, A.ohT_ps, A.ohT_sb, A.q_done, A.t1, A.t2, A.seg):
                V.sem_inc(s_, 2)

            prep = Steps(s_prep)
            dve.wait_ge(s_in_e, 32)
            prep(V.tensor_copy(dst_f[:, :], dst_all[:, :]))
            prep(V.tensor_reduce(cmin[:, 0:C], dst_f[:, :].rearrange("p (c t) -> p c t", t=CT), AX, ALU.min))
            prep(V.scalar_tensor_tensor(out=slot0[:, :], in0=dst_f[:, :], scalar=float(PAD_DST), in1=dst_f[:, :],
                                        op0=ALU.is_lt, op1=ALU.mult))
            prep(V.tensor_reduce(cmin[:, C:2 * C], slot0[:, :].rearrange("p (c t) -> p c t", t=CT), AX, ALU.max))
            dve.wait_ge(s_prep_pe, 1)
            prep(V.tensor_reduce(cred[:, 0:1], bank[0][0:C, 0:P], AX, ALU.min))
            prep(V.tensor_reduce(cred[:, 1:2], bank[1][0:C, 0:P], AX, ALU.max))
            for m in range(2):
                prep(V.tensor_copy(cwide[:, m, :], cred[:, m:m + 1].broadcast_to([C, P])))
            dve.wait_ge(s_prep_pe, 2)
            prep(V.tensor_copy(base0[:, :], bank[2][:, 0:C]))
            prep(V.tensor_tensor(span_f[:, :], bank[3][0:1, 0:C], base0[0:1, :], ALU.subtract))
            prep(V.tensor_reduce(span_m[:, :], span_f[:, :], AX, ALU.max))
            prep(V.tensor_tensor(slot0[:, :].rearrange("p (c t) -> p c t", t=CT),
                                 dst_f[:, :].rearrange("p (c t) -> p c t", t=CT),
                                 base0[:, :].unsqueeze(2).broadcast_to([P, C, CT]), ALU.subtract))
            prep(V.memset(base_i[:, :], 0))
            V.tensor_copy(span_i[:, :], span_m[:, :]).then_inc(s_base, 1)
            prep(V.memset(ones[:, :], 1.0))
            prep(V.tensor_scalar(first_f[:, :], dst_f[0:1, :].rearrange("p (c t) -> p c t", t=BT)[:, :, 0], float(n_nodes),
                                 None, ALU.min))
            dve.wait_ge(s_ident, 1)
            prep(V.tensor_copy(ident_b[:, :], ident[:, :]))
            prep(V.tensor_copy(iota_f[:, :], iota_i[:, :]))
            prep(V.tensor_copy(iota_h[:, :], key_i[:, :]))
            prep(V.memset(zero_b[:, :], 0.0))
            prep(V.memset(xT[D:D + 1, :, :], 1.0))
            prep(V.tensor_scalar(dst_all[:, :], src_all[:, :], P - 1, None, ALU.bitwise_and))
            prep(V.tensor_scalar(src_all[:, :], src_all[:, :], 7, None, ALU.logical_shift_right))
            prep(V.tensor_copy(lo_f[:, :], dst_all[:, :]))
            prep(V.tensor_copy(lo_h[:, :], dst_all[:, :]))
            prep(V.tensor_copy(iota_6[:, :, :], iota_f[:, :].unsqueeze(2).broadcast_to([P, P, 2 * BT])))
            dve.wait_ge(s_prep_pe, 3)
            prep(V.memset(first_i[:, :], 0))
            prep(V.tensor_copy(first_i[:, 0:BC], first_f[:, :]))
            prep(V.tensor_tensor(key[:, :].rearrange("p (c t) -> p c t", t=BT),
                                 dst_f[:, :].rearrange("p (c t) -> p c t", t=BT),
                                 bank[4][:, 0:BC].unsqueeze(2).broadcast_to([P, BC, BT]), ALU.subtract))
            tile_before = dst_f[:, :].rearrange("p (c t) -> p c t", t=BT)[:, 0:BC - 1, BT - 1]
            prep(V.memset(carry[:, :], float(PAD_DST)))
            prep(V.tensor_tensor(carry[:, 1:BC], tile_before, bank[4][:, 1:BC], ALU.not_equal))
            prep(V.scalar_tensor_tensor(out=carry[:, 1:BC], in0=carry[:, 1:BC], scalar=float(PAD_DST),
                                        in1=src_all[:, :].rearrange("p (c t) -> p c t", t=BT)[:, 0:BC - 1, BT - 1],
                                        op0=ALU.mult, op1=ALU.add))
            prep(V.tensor_copy(carry_h[:, :], carry[:, :]))
            prep(V.tensor_copy(iota_c[:, :, 0], iota_f[:, 0:NH]))
            prep(V.tensor_scalar(dst_f[:, :], key[:, :], float(SW), float(PAD_DST), ALU.is_ge, ALU.mult))
            prep(V.tensor_tensor(dst_f[:, :], dst_f[:, :], key[:, :], ALU.add))
            prep(V.tensor_scalar(key[:, :], key[:, :], 0.0, float(PAD_DST), ALU.is_lt, ALU.mult))
            prep(V.tensor_tensor(dst_f[:, :], dst_f[:, :], key[:, :], ALU.add))
            prep(V.scalar_tensor_tensor(out=key[:, :], in0=src_all[:, :], scalar=float(SW), in1=dst_f[:, :],
                                        op0=ALU.mult, op1=ALU.add))

            def onehot(dst, width, vals, at):
                return V.tensor_tensor(dst, iota_f[:, 0:width].unsqueeze(1).broadcast_to([P, G, width]),
                                       vals[:, bass.ds(at, G)].unsqueeze(2).broadcast_to([P, G, width]), ALU.is_equal)

            def window_onehots(c, w):
                dve.wait_ge(b_mm, c + 1)
                if w % 2 == 0:
                    V.tensor_tensor(lo_oh[:, w // 2, :, :], iota_6[:, :, :],
                                    lo_h[:, bass.ds(c * BT, 2 * BT)].unsqueeze(1).broadcast_to([P, P, 2 * BT]), ALU.is_equal)
                for t in range(BT):
                    last = V.tensor_scalar(key_oh[:, w % BR, t, :], iota_h[:, :], key[:, bass.ds(c * BT + t, 1)], None,
                                           ALU.is_equal)
                last.then_inc(b_oh, 1)

            st = prep
            st(V.memset(lo_oh[:, BR - 1, :, :], 0.0))
            st(V.tensor_tensor(carry_oh, iota_c[:, :, :].broadcast_to([P, NH, BC]),
                               carry_h[:, :].unsqueeze(1).broadcast_to([P, NH, BC]), ALU.is_equal))
            dve.wait_ge(b_clear, 1)
            with dve.Fori(0, BC // (2 * BR)) as i:
                for w in range(2 * BR):
                    window_onehots(i * (2 * BR) + w, w)
            for w in range(BC % (2 * BR)):
                window_onehots(BC // (2 * BR) * (2 * BR) + w, w)
            dve.wait_ge(b_wr, BC + BR)

            def split(src, rest, st):
                st(V.tensor_copy(parts[:, :, HIGH:HIGH + D], src))
                st(V.tensor_tensor(rest, src, parts[:, :, HIGH:HIGH + D], ALU.subtract))
                st(V.tensor_copy(parts[:, :, MID:MID + D], rest))
                st(V.tensor_tensor(rest, rest, parts[:, :, MID:MID + D], ALU.subtract))
                st(V.tensor_copy(parts[:, :, LOW:LOW + D], rest))

            def dense(m, src, st):
                split(src, agg[:, :, 0:D], st)
                st(V.memset(agg[:, NH:NB, :], 0.0))
                st(V.memset(parts[:, :, ONE:ONE + 1], 1.0))
                V.sem_inc(d_go, 1)

                def convert(b, u):
                    dve.wait_ge(d_mm, b + (m * NH + 1))
                    V.tensor_copy(block_b[:, u, ACT_H:NH, :], counts[:, ACT_H:NH, bass.ds(b * P, P)]).then_inc(d_cv, 1)

                def evict(b, u):
                    n = b + m * NH
                    row = agg[:, bass.ds(b, 1), 0:D].rearrange("p o d -> p (o d)")
                    dve.wait_ge(d_mm, n + 3)
                    dve.wait_ge(d_ea, n + 1)
                    V.tensor_tensor(row, row, N_o[u][:, MID:MID + D], ALU.add).then_inc(d_st, 1)
                    dve.wait_ge(d_st, n + 1)
                    V.tensor_tensor(row, row, N_o[u][:, LOW:LOW + D], ALU.add).then_inc(d_ev, 1)

                convert(0, 0)
                with dve.Fori(0, NH // 2) as i:
                    for u in range(2):
                        convert(i * 2 + (u + 1), 1 - u)
                        evict(i * 2 + u, u)
                evict(NH - 1, 0)
                dve.wait_ge(d_ev, (m + 1) * NH + 2)

            def out_degrees():
                st = Steps(deg_step)
                st(V.tensor_scalar(slot[:, :], slot0[:, :], float(n_nodes), float(PAD_DST), ALU.is_ge, ALU.mult))
                st(V.tensor_tensor(slot[:, :], slot[:, :], src_all[:, :], ALU.add))
                V.sem_inc(s_deg_oh, 1)
                V.sem_inc(s_deg_mm, 2)
                with dve.Fori(0, NT // (2 * G)) as i:
                    for u in range(2):
                        dve.wait_ge(s_deg_mm, i * 2 + u + 1)
                        onehot(oh_b[:, u, :, :], P, lo_f, (i * 2 + u) * G)
                        onehot(oh_hi[:, u, :, :], NB, slot, (i * 2 + u) * G).then_inc(s_deg_oh, 1)
                dve.wait_ge(s_deg_mm, NT // G + 2)
                st(V.tensor_scalar(outdeg[:, :], bank[7][:, 0:NB], 1.0, None, ALU.max))

            npass = passes(dve)

            def start_pass_state(k):
                a = L[k]
                st = Steps(a.step)
                st(V.tensor_copy(slot[:, :], slot0[:, :]))
                st(V.tensor_copy(base_f[:, :], base0[0:1, :]))
                return st

            def open_pass(k, p):
                a = L[k]
                st = Steps(a.step, p * 4 + 3)
                st(V.tensor_scalar(base_i[0:1, 1:C + 1], base_f[:, :], float(LAST_BASE), None, ALU.min))
                st(V.memset(flush[:, :], 0.0))
                V.sem_inc(a.pass_ready, 1)
                V.sem_inc(a.flush_ready, 1)

            def close_pass(k, p):
                dve.wait_ge(L[k].flushed, (p + 1) * (16 * (C + 1)))
                st = Steps(L[k].step, p * 4 + 5)
                st(V.tensor_scalar(slot[:, :], slot[:, :], float(-P), None, ALU.add))
                st(V.tensor_scalar(base_f[:, :], base_f[:, :], float(P), None, ALU.add))

            def copy_window(a, p, c, n, w):
                dve.wait_ge(a.flushed, (p * (C + 1) + c + 1) * 16)
                V.tensor_copy(flush[:, 0:w], acc[:, 0:w]).then_inc(a.flush_ready, 1)

            def aggregate(k):
                a = L[k]
                pass_state = start_pass_state(k)
                pass_state(V.memset(kv[:, :, :, D:WA], 1.0))
                V.sem_inc(a.go, 1)
                with dve.Fori(0, npass) as p:
                    open_pass(k, p)
                    with dve.Fori(0, C) as c:
                        it = dve.snap(p * C + c)
                        for g in range(CG):
                            dve.wait_ge(a.used, it * CG + g + KV_RING)
                            onehot(oh[:, g % 2, :, :], P, slot, c * CT + g * G).then_inc(a.oh_ready, 1)
                        dve.wait_ge(a.used, (it + 1) * CG + USED0)
                        copy_window(a, p, c, it, WA)
                    close_pass(k, p)

            roots = [0]

            def root(ins):
                roots[0] += 1
                ins.then_inc(s_sqrt_in, 1)
                dve.wait_ge(s_sqrt, roots[0])

            def layer_norm(y, dst):
                wide = stat[:, 0, :].unsqueeze(2).broadcast_to([P, NB, D])
                st(V.tensor_reduce(stat[:, 0, :], y, AX, ALU.add))
                st(V.tensor_scalar(stat[:, 0, :], stat[:, 0, :], 1.0 / D, None, ALU.mult))
                st(V.tensor_tensor(y, y, wide, ALU.subtract))
                st(V.tensor_tensor(sq, y, y, ALU.mult))
                st(V.tensor_reduce(stat[:, 1, :], sq, AX, ALU.add))
                root(V.tensor_scalar(stat[:, 2, :], stat[:, 1, :], 1.0 / D, 1e-5, ALU.mult, ALU.add))
                st(V.reciprocal(stat[:, 3, :], stat[:, 2, :]))
                st(V.tensor_tensor(dst, y, stat[:, 3, :].unsqueeze(2).broadcast_to([P, NB, D]), ALU.mult))

            def node(m, n_out, evict):
                with dve.Fori(0, NB // 2) as i:
                    for u in range(2):
                        dve.wait_ge(n_mm, i * 2 + (u + m * NB + 3))
                        evict(i * 2 + u, N_o[u]).then_inc(n_ev, 1)
                dve.wait_ge(n_ev, (m + 1) * NB + 2)

            st = Steps(n_step)

            def blk(t, b, w=D):
                return t[:, bass.ds(b, 1), 0:w].rearrange("p o d -> p (o d)")

            def dense_or_edges(k, m):
                with dve.If(bad):
                    aggregate(k)
                    dve.wait_ge(sums_loaded[k], 16)
                with dve.Else():
                    dense(m, ya[:, :, :], Steps(d_parts, 7 * (m - 1)))

            dve.wait_ge(s_in_x, 16)
            dve.wait_ge(s_zeroed, 64)
            dense(0, xa[:, :, :], st)
            V.reduce_sum(degsum[:, :], agg[:, :, D:WA].rearrange("p b o -> p (b o)"), AX).then_inc(s_degsum, 1)
            dve.wait_ge(s_total, 1)
            st(V.tensor_scalar(bad_f[:, :], bank[4][0:1, 0:1], float(n_edges), None, ALU.not_equal))
            V.tensor_copy(bad_i[:, :], bad_f[:, :]).then_inc(s_bad, 1)
            bad = load_bad(dve)
            with dve.If(bad):
                aggregate(0)
                dve.wait_ge(sums_loaded[0], 16)
            st(V.tensor_scalar(indeg[:, :], agg[:, :, D:WA].rearrange("p b o -> p (b o)"), 1.0, None, ALU.max))
            root(V.tensor_copy(dinv_in[:, :], indeg[:, :]))
            st(V.reciprocal(dinv_in[:, :], dinv_in[:, :]))
            st(V.reciprocal(stat[:, 0, :], indeg[:, :]))
            dve.wait_ge(s_in_x, 16)
            V.tensor_tensor(agg[:, :, 0:D], agg[:, :, 0:D], stat[:, 0, :].unsqueeze(2).broadcast_to([P, NB, D]),
                            ALU.mult).then_inc(n_go, 1)
            node(0, D, lambda b, ps: V.tensor_tensor(blk(ya, b), blk(xa, b), ps[:, 0:D], ALU.add))
            layer_norm(ya[:, :, :], xa[:, :, :])
            V.sem_inc(n_go, 1)

            node(1, 3 * D, lambda b, ps: V.tensor_copy(blk(kvq, b, 3 * D), ps[:, 0:3 * D]))
            q = kvq[:, :, 2 * D:3 * D]
            st(V.tensor_scalar(q, q, QSCALE, None, ALU.mult))
            split(q, q, st)
            V.sem_inc(s_kvq, 1)

            a = A
            pass_state = start_pass_state(1)
            dve.wait_ge(s_stored, 32)
            pass_state(V.memset(ea[D:D + 1, :, :], 1.0))
            V.sem_inc(a.go, 1)

            def scores(it, g):
                u, r, n = g % 2, g % KV_RING, it * CG + g
                dve.wait_ge(a.e_done, n + KV_RING + 1)
                dve.wait_ge(a.gathered[r], (it * 2 + g // KV_RING + 1) * (16 * G))
                pr = prod[:, u, :].rearrange("p (g d) -> p g d", g=G)
                V.tensor_tensor(pr, kv[:, r, :, 0:D], E_ps[u][:, 0:G * D].rearrange("p (g d) -> p g d", g=G),
                                ALU.mult).then_inc(a.t1, 1)

            def reduce_scores(it, g):
                u, n = g % 2, it * CG + g
                dve.wait_ge(a.q_done, n + 3)
                dve.wait_ge(a.t1, n + 3)
                V.tensor_tensor(prod[:, u, :], prod[:, u, :], Q_ps[u][:, 0:G * D], ALU.mult).then_inc(a.t2, 1)
                dve.wait_ge(a.t2, n + 3)
                V.tensor_reduce(sc[:, u, :], prod[:, u, :].rearrange("p (s d) -> p s d", d=HD), AX,
                                ALU.add).then_inc(a.red, 1)
                dve.wait_ge(a.red, n + 1)
                V.tensor_scalar(sc[:, u, :], sc[:, u, :], -5.0, 5.0, ALU.max, ALU.min).then_inc(a.sc, 1)

            def messages(it, g):
                u, r, n = g % 2, g % KV_RING, it * CG + g
                dve.wait_ge(a.exp, n + 1)
                w = msg[:, u, :, D:WT].unsqueeze(3).broadcast_to([P, G, H, HD])
                V.tensor_tensor(msg[:, u, :, 0:D].rearrange("p g (h d) -> p g h d", h=H),
                                kv[:, r, :, D:2 * D].rearrange("p g (h d) -> p g h d", h=H), w,
                                ALU.mult).then_inc(a.used, 1)

            def slots(it, c, g):
                n = it * CG + g
                dve.wait_ge(a.ohT_ps, n + 1)
                dve.wait_ge(a.oh32, n + 1)
                onehot(oh_b[:, g % 2, :, :], P, slot, c * CT + g * G).then_inc(a.oh_ready, 1)

            PIECES = 3
            SLICE = -(-n_nodes // (C * PIECES))

            def out_degree_piece(p, c, k):
                V.tensor_reduce(outpart[:, :], counts[:, :, bass.ds(c * (PIECES * SLICE) + k * SLICE, SLICE)], AX,
                                ALU.add).then_inc(s_outdeg, 1)
                dve.wait_ge(s_outdeg, p * (2 * PIECES * C + 1) + c * (2 * PIECES) + (2 * k + 2))
                V.tensor_tensor(outdeg[:, 0:NH], outdeg[:, 0:NH], outpart[:, :], ALU.add).then_inc(s_outdeg, 1)

            with dve.Fori(0, npass) as p:
                open_pass(1, p)
                V.memset(outdeg[:, :], 0.0).then_inc(s_outdeg, 1)
                with dve.Fori(0, C) as c:
                    it = dve.snap(p * C + c)
                    slots(it, c, 0)
                    for g in range(CG):
                        scores(it, g)
                        if g:
                            messages(it, g - 1)
                        if g + 1 < CG:
                            slots(it, c, g + 1)
                        if 1 <= g <= PIECES:
                            out_degree_piece(p, c, g - 1)
                        reduce_scores(it, g)
                    messages(it, CG - 1)
                close_pass(1, p)

            dve.wait_ge(sums_loaded[1], 16)
            with dve.If(bad):
                out_degrees()
            root(V.tensor_scalar(dinv_out[:, :], outdeg[:, :], 1.0, None, ALU.max))
            st(V.reciprocal(dinv_out[:, :], dinv_out[:, :]))
            st(V.tensor_scalar(agg[:, :, D:WT], agg[:, :, D:WT], 1e-6, None, ALU.add))
            st(V.reciprocal(agg[:, :, D:WT], agg[:, :, D:WT]))
            for h in range(H):
                st(V.tensor_tensor(agg[:, :, h * HD:(h + 1) * HD], agg[:, :, h * HD:(h + 1) * HD],
                                   agg[:, :, D + h:D + h + 1].broadcast_to([P, NB, HD]), ALU.mult))
            st(V.tensor_tensor(ya[:, :, :], agg[:, :, 0:D], xa[:, :, :], ALU.add))
            layer_norm(ya[:, :, :], xa[:, :, :])
            V.tensor_tensor(ya[:, :, :], xa[:, :, :], dinv_out[:, :].unsqueeze(2).broadcast_to([P, NB, D]),
                            ALU.mult).then_inc(s_t2, 1)
            dve.wait_ge(s_t2, 1)

            dense_or_edges(2, 1)
            V.tensor_tensor(agg[:, :, 0:D], agg[:, :, 0:D], dinv_in[:, :].unsqueeze(2).broadcast_to([P, NB, D]),
                            ALU.mult).then_inc(n_go, 1)
            node(2, D, lambda b, ps: V.tensor_tensor(blk(ya, b), blk(xa, b), ps[:, 0:D], ALU.add))
            layer_norm(ya[:, :, :], xa[:, :, :])
            V.sem_inc(n_go, 1)

            def evict3(b, ps):
                V.tensor_copy(blk(r3, b), ps[:, D:2 * D])
                return V.tensor_copy(blk(ya, b), ps[:, 0:D])

            node(3, 2 * D, evict3)
            V.tensor_tensor(ya[:, :, :], ya[:, :, :], dinv_in[:, :].unsqueeze(2).broadcast_to([P, NB, D]),
                            ALU.mult).then_inc(s_t3, 1)
            dve.wait_ge(s_t3, 1)
            dense_or_edges(3, 2)
            st(V.tensor_tensor(ya[:, :, :], agg[:, :, 0:D], dinv_in[:, :].unsqueeze(2).broadcast_to([P, NB, D]), ALU.mult))
            st(V.tensor_tensor(ya[:, :, :], ya[:, :, :], r3, ALU.add))
            st(V.tensor_scalar(ya[:, :, :], ya[:, :, :], 0.0, None, ALU.max))
            st(V.tensor_tensor(ya[:, :, :], ya[:, :, :], xa[:, :, :], ALU.add))
            layer_norm(ya[:, :, :], xa[:, :, :])
            V.sem_inc(s_final, 1)


def kernel(x, src, dst, edge_attr_96, L0_gnn_W_self, L0_gnn_W_neigh, L0_gnn_b, L1_gnn_Wq, L1_gnn_bq, L1_gnn_Wk, L1_gnn_bk,
           L1_gnn_We, L1_gnn_be, L1_gnn_Wv, L1_gnn_bv, L2_gnn_weight, L2_gnn_bias, L3_gnn_W_lin, L3_gnn_b_lin,
           L3_gnn_W_root, L3_gnn_b_root):
    import numpy as np
    import concourse.bacc as bacc
    from concourse import mybir as mb
    from concourse.bass_utils import run_bass_kernel_spmd

    P, NR, NT, E, N = 128, 26 * 128, 810, 103125, 3125
    A = np.asarray

    def edges(a, fill):
        padded = np.full((NT * P,), fill, np.int32)
        padded[:E] = A(a)
        return np.ascontiguousarray(padded.reshape(NT, P).T)

    def with_bias(w, b):
        return np.ascontiguousarray(np.concatenate([A(w), A(b)[None, :]], axis=0))

    x_pad = np.zeros((NR, 96), np.float32)
    x_pad[:N] = A(x)
    ea_t = np.zeros((96, NT * P), np.float32)
    ea_t[:, :E] = A(edge_attr_96).T
    arrays = {
        "x_in": x_pad,
        "src_in": edges(src, 0),
        "dst_in": edges(dst, 1 << 20),
        "ea_in": ea_t,
        "w_self": with_bias(L0_gnn_W_self, L0_gnn_b),
        "w_neigh": np.ascontiguousarray(A(L0_gnn_W_neigh)),
        "w_kvq": np.concatenate([with_bias(L1_gnn_Wk, L1_gnn_bk), with_bias(L1_gnn_Wv, L1_gnn_bv),
                                 with_bias(L1_gnn_Wq, L1_gnn_bq)], axis=1),
        "w_edge": with_bias(L1_gnn_We, L1_gnn_be),
        "w_gcn": with_bias(L2_gnn_weight, L2_gnn_bias),
        "w_lin_root": np.concatenate([with_bias(A(L3_gnn_W_lin).T, L3_gnn_b_lin),
                                      with_bias(A(L3_gnn_W_root).T, L3_gnn_b_root)], axis=1),
    }
    nc = bacc.Bacc("TRN2", target_bir_lowering=False, num_devices=1)
    args = [nc.dram_tensor(n, list(a.shape), mb.dt.from_np(a.dtype), kind="ExternalInput").ap() for n, a in arrays.items()]
    out = nc.dram_tensor("out", [N, 96], mb.dt.float32, kind="ExternalOutput").ap()
    residual_gnn_kernel(nc, *args, out, N, E)
    r = run_bass_kernel_spmd(nc, [arrays], core_ids=[0])
    return r.results[0]["out"]
```

```python
import concourse.bass as bass
from concourse import mybir
from contextlib import ExitStack


def residual_gnn_kernel(nc, x_in, src_in, dst_in, ea_in, w_self, w_neigh, w_kvq, w_edge, w_gcn, w_lin_root, out, n_nodes, n_edges):
    fp32, bf16, i32 = mybir.dt.float32, mybir.dt.bfloat16, mybir.dt.int32
    fp16, u8 = mybir.dt.float16, mybir.dt.uint8
    ALU, ACT, AX = mybir.AluOpType, mybir.ActivationFunctionType, mybir.AxisListType.X

    P = 128
    D = 96
    H = 8
    HD = D // H
    NB = x_in.shape[0] // P
    NR = NB * P
    NT = src_in.shape[1]
    G = 5
    CG = 6
    CT = G * CG
    C = NT // CT
    HT = CT // 2
    KV_RING = 3
    USED0 = KV_RING + 1
    QSCALE = float(HD) ** -0.5
    PAD_DST = 1 << 20
    LAST_BASE = NR - P
    PASSES_MAX = (n_nodes - 1) // P + 1
    NH = (n_nodes + P - 1) // P
    SW = 16
    BT = 3
    BC = NT // BT
    NP = NB // 2
    KV_PIECES = 4
    KEYS = NH * SW
    ACT_H = 15

    ctx = ExitStack()
    with ctx:
        def sb(name, shape, dt=fp32):
            return ctx.enter_context(nc.sbuf_tensor(name, shape, dt))

        def pb(name, shape, dt=fp32):
            return ctx.enter_context(nc.psum_tensor(name, shape, dt))

        def sem(name):
            return ctx.enter_context(nc.semaphore(name))

        kv_tab = nc.dram_tensor("kv_tab", [NR, 2 * D], fp32, kind="Internal").ap()
        q_tab = nc.dram_tensor("q_tab", [NR, 3 * D], bf16, kind="Internal").ap()
        t2_tab = nc.dram_tensor("t2_tab", [NR, D], fp32, kind="Internal").ap()
        t3_tab = nc.dram_tensor("t3_tab", [NR, D], fp32, kind="Internal").ap()
        WA = D + 1
        WT = D + H
        sums = {0: nc.dram_tensor("sum0", [NR, WA], fp32, kind="Internal").ap(),
                1: nc.dram_tensor("sum1", [NR, WT], fp32, kind="Internal").ap(),
                2: nc.dram_tensor("sum2", [NR, WA], fp32, kind="Internal").ap(),
                3: nc.dram_tensor("sum3", [NR, WA], fp32, kind="Internal").ap()}
        tables = {0: x_in, 2: t2_tab, 3: t3_tab}

        def rows(ap):
            return ap.rearrange("(b p) d -> p b d", p=P)

        ident = sb("ident", [P, P])
        ident_b = sb("ident_b", [P, P], bf16)
        iota_i = sb("iota_i", [P, P], i32)
        iota_f = sb("iota_f", [P, P])
        key_i = sb("key_i", [P, KEYS], i32)
        iota_h = sb("iota_h", [P, KEYS], fp16)
        ones = sb("ones", [P, P])
        iota_6 = sb("iota_6", [P, P, 2 * BT], bf16)
        lo_h = sb("lo_h", [P, NT], bf16)
        zero_b = sb("zero_b", [P, P], bf16)
        first_f = sb("first_f", [1, BC])
        first_i = sb("first_i", [1, BC + 2], i32)
        degsum = sb("degsum", [P, 1])
        bad_f = sb("bad_f", [1, 1])
        bad_i = sb("bad_i", [1, 1], i32)
        carry = sb("carry", [P, BC])
        carry_h = sb("carry_h", [P, BC], bf16)
        outpart = sb("outpart", [P, NH])
        src_all = sb("src_all", [P, NT], i32)
        dst_all = sb("dst_all", [P, NT], i32)
        dst_f = sb("dst_f", [P, NT])
        slot0 = sb("slot0", [P, NT])
        slot = sb("slot", [P, NT])
        key = slot
        cmin = sb("cmin", [P, 2 * C])
        cred = sb("cred", [C, 2])
        cwide = sb("cwide", [C, 2, P])
        base0 = sb("base0", [P, C])
        base_f = sb("base_f", [1, C])
        base_i = sb("base_i", [1, C + 1], i32)
        span_f = sb("span_f", [1, C])
        span_m = sb("span_m", [1, 1])
        span_i = sb("span_i", [1, 1], i32)

        xa = sb("xa", [P, NB, D])
        ya = sb("ya", [P, NB, D])
        agg = sb("agg", [P, NB, WT])
        stat = sb("stat", [P, 6, NB])
        outdeg = sb("outdeg", [P, NB])
        indeg = sb("indeg", [P, NB])
        dinv_out = sb("dinv_out", [P, NB])
        dinv_in = sb("dinv_in", [P, NB])
        parts = sb("parts", [P, NB, 3 * D + 2], bf16)
        MID, LOW, HIGH, ONE = 0, D, 2 * D, 3 * D
        counts = sb("counts", [P, NH, NH * P], u8)

        area = sb("area", [P, NB * 3 * D])
        kv_new = area[:, 0:NB * 2 * D].rearrange("p (b d) -> p b d", d=2 * D)
        at = 0

        def carve(n):
            nonlocal at
            at += n
            return area[:, at - n:at]

        kv = carve(KV_RING * G * 2 * D).rearrange("p (r g d) -> p r g d", r=KV_RING, g=G)
        oh = carve(2 * G * P).rearrange("p (u g n) -> p u g n", u=2, g=G)
        ea = carve(KV_RING * G * P).rearrange("p (r n) -> p r n", r=KV_RING)
        prod = carve(2 * G * D).rearrange("p (u n) -> p u n", u=2)
        r3 = area[:, (KV_RING * 2 * D + 2 * P) * G:][:, 0:NB * D].rearrange("p (b d) -> p b d", d=D)
        block_b = area[:, 0:NH * P].bitcast(bf16).rearrange("p (u h n) -> p u h n", u=2, h=NH)
        BR = 4
        key_oh = area[:, 0:BR * BT * KEYS // 2].bitcast(bf16).rearrange("p (u t n) -> p u t n", u=BR, t=BT)
        lo_oh = area[:, BR * BT * KEYS // 2:][:, 0:BR * BT * P].bitcast(bf16).rearrange("p (u n t) -> p u n t", u=BR, n=P)
        carry_oh = area[:, BR * BT * (KEYS // 2 + P):][:, 0:NH * BC // 2].bitcast(bf16).rearrange("p (h c) -> p h c", h=NH)

        w_self_t = sb("w_self_t", [D + 1, D])
        w_neigh_t = sb("w_neigh_t", [D, D])
        w_kvq_t = sb("w_kvq_t", [D + 1, 3 * D])
        w_edge_t = sb("w_edge_t", [D + 1, D])
        w_gcn_t = sb("w_gcn_t", [D + 1, D])
        w_lr_t = sb("w_lr_t", [D + 1, 2 * D])

        xs = sb("xs", [P, 2, 4, D])
        xT = sb("xT", [D + 1, 2, 4 * P])
        bn = sb("bn", [P, NB, 6])

        idx = sb("idx", [P, 2, HT], i32)
        oh_b = sb("oh_b", [P, 2, G, P], bf16)
        ohT = sb("ohT", [P, 2, G, P], bf16)
        q_land = sb("q_land", [P, 3 * D], bf16)
        q_win = sb("q_win", [P, 3 * D], bf16)
        sc = sb("sc", [P, 2, G * H])
        msg = sb("msg", [P, 2, G, WT])
        flush = sb("flush", [P, WT])

        lo_f = dst_f
        oh_hi = sb("oh_hi", [P, 2, G, NB], bf16)

        bank = [pb(f"bank{i}", [P, 512]) for i in range(8)]
        E_ps = [bank[0], bank[1]]
        Q_ps = [bank[2], bank[3]]
        T_ps = [bank[4][:, :].bitcast(bf16), bank[5][:, :].bitcast(bf16)]
        acc = bank[6]
        N_t = [bank[0], bank[1]]
        N_o = [bank[2], bank[3]]
        N_4 = [bank[2], bank[3], bank[6], bank[7]]
        N_2 = [bank[4], bank[5]]

        s_in_x, s_in_e, s_in_w, s_zeroed = sem("in_x"), sem("in_e"), sem("in_w"), sem("zeroed")
        s_zeros = sem("zeros_ready")
        s_pool = sem("pool_step")
        s_ident = sem("ident_ready")
        s_prep = sem("prep_step")
        s_prep_pe = sem("prep_transposed")
        s_base = sem("bases_ready")
        s_deg_oh, s_deg_mm = sem("deg_onehot"), sem("deg_summed")
        b_clear, b_oh, b_mm, b_wr = (sem("counts_clear"), sem("window_onehot"), sem("window_summed"),
                                            sem("window_written"))
        d_go, d_cv, d_ca, d_mm, d_ea, d_st, d_ev = (sem("dense_parts"), sem("dense_block_dve"), sem("dense_block_act"),
                                              sem("dense_product"), sem("dense_high_part"), sem("dense_mid_part"), sem("dense_evicted"))
        s_degsum, s_total, s_bad = sem("degree_sums"), sem("total"), sem("bad_known")
        s_outdeg = sem("outdeg_step")
        deg_step = sem("outdeg_dve_step")
        s_tab2, s_tab3 = sem("t2_stored"), sem("t3_stored")

        block = ctx.enter_context(nc.Block())

        class Agg:
            def __init__(self, k):
                n = f"L{k}_"
                self.idx_ready = [sem(n + f"idx_ready{i}") for i in range(2)]
                self.gathered = [sem(n + f"gathered{i}") for i in range(KV_RING)]
                self.used = sem(n + "used")
                self.oh_ready = sem(n + "onehot")
                self.chunk_summed = sem(n + "chunk_summed")
                self.flush_ready = sem(n + "flush_ready")
                self.flushed = sem(n + "flushed")
                self.pass_ready = sem(n + "pass_ready")
                self.go = sem(n + "table_ready")
                self.step = sem(n + "dve_step")

        L = {k: Agg(k) for k in range(4)}
        A = L[1]
        A.q_ready, A.qwin = sem("L1_q_loaded"), sem("L1_q_window")
        A.ea_ready = [sem(f"L1_ea_ready{i}") for i in range(KV_RING)]
        A.e_done, A.ohT_ps, A.ohT_sb, A.q_done = sem("L1_e"), sem("L1_ohT_ps"), sem("L1_ohT_sb"), sem("L1_q")
        A.oh32, A.t1, A.t2, A.red, A.sc, A.exp, A.seg = (sem("L1_oh32"), sem("L1_t1"), sem("L1_t2"), sem("L1_red"),
                                                         sem("L1_scores"), sem("L1_exp"), sem("L1_segment"))

        n_go, n_staged, n_tr, n_xT = sem("node_input"), sem("node_staged"), sem("node_transposed"), sem("node_xT")
        n_mm, n_ev, n_step = sem("node_product"), sem("node_evicted"), sem("node_dve_step")
        n_ea, n_bn, n_split = sem("node_evicted_act"), sem("node_statistics"), sem("node_split_step")
        s_kv_stored, s_q_stored = sem("kv_rows_stored"), sem("q_rows_stored")
        s_pool_split, d_free = sem("pool_split_step"), sem("dense_area_free")
        s_norm_in, s_norm = sem("norm_input"), sem("norm_act_done")
        NL = 18
        sums_half = [sem("sums1_first_half"), sem("sums1_second_half")]
        s_split, s_split_act = sem("split_dve_step"), sem("split_act_step")
        d_tail, s_scaled = sem("dense_residual"), sem("edge_sums_scaled")
        SPLIT = 4
        s_sqrt_in, s_sqrt = sem("sqrt_input"), sem("sqrt_done")
        s_t2, s_t3, s_final = sem("t2_ready"), sem("t3_ready"), sem("final_ready")
        s_stored = sem("stored")
        s_waited = sem("waited")
        sums_whole = [sem(f"sums{k}_whole") for k in range(4)]
        sums_loaded = [sem(f"sums{k}_loaded") for k in range(4)]

        def passes(eng):
            eng.wait_ge(s_base, 1)
            span = eng.value_load(span_i[0:1, 0:1], min_val=0, max_val=n_nodes - 1)
            return eng.snap(span // P + 1, min_val=1, max_val=PASSES_MAX)

        def load_bad(eng):
            eng.wait_ge(s_bad, 1)
            return eng.value_load(bad_i[0:1, 0:1], min_val=0, max_val=1)

        def load_firsts(eng, c):
            return nc.values_load_multi_w_load_instructions(first_i[0:1, bass.ds(c, BR)], engines=[eng.engine],
                                                            min_val=0, max_val=n_nodes)[1]

        def wait_alone(eng, s, value):
            eng.wait_ge(s, value)
            eng.sem_inc(s_waited, 1)

        @block.sync
        def _(sp):
            sp.dma_start(dst_all[:, :], dst_in).then_inc(s_in_e, 16)
            sp.dma_start(src_all[:, :], src_in).then_inc(s_in_e, 16)
            sp.dma_start(xa[:, :, :], rows(x_in)).then_inc(s_in_x, 16)
            for t, w in ((w_self_t, w_self), (w_neigh_t, w_neigh), (w_kvq_t, w_kvq), (w_edge_t, w_edge),
                         (w_gcn_t, w_gcn), (w_lr_t, w_lin_root)):
                sp.dma_start(t[:, :], w).then_inc(s_in_w, 16)
            sp.wait_ge(s_zeros, 1)
            for k in range(4):
                w = sums[k].shape[1]
                sp.dma_start(sums[k].rearrange("(p b) d -> p (b d)", p=P),
                             agg[:, :, :].rearrange("p b d -> p (b d)")[:, 0:NB * w]).then_inc(s_zeroed, 16)
            npass = passes(sp)

            def load_idx(a, it, c, h):
                sp.wait_ge(a.used, it * CG + h * (CG // 2) + 1)
                sp.dma_start(idx[:, h, :], src_in[:, bass.ds(c * CT + h * HT, HT)]).then_inc(a.idx_ready[h], 16)

            def aggregate(k):
                a = L[k]
                with sp.Fori(0, npass) as p:
                    with sp.Fori(0, C) as c:
                        it = sp.snap(p * C + c)
                        for h in range(2):
                            load_idx(a, it, c, h)

            def attention():
                a = A
                with sp.Fori(0, npass) as p:
                    wait_alone(sp, a.pass_ready, p + 1)
                    with sp.Fori(0, C) as c:
                        it = sp.snap(p * C + c)
                        load_idx(a, it, c, 0)
                        b = sp.value_load(base_i[0:1, bass.ds(c + 1, 1)], min_val=0, max_val=LAST_BASE)
                        sp.wait_ge(a.qwin, it + 1)
                        sp.wait_ge(s_q_stored, 32)
                        sp.dma_start(q_land[:, :], q_tab[bass.ds(b, P), :]).then_inc(a.q_ready, 16)
                        for g in range(CG):
                            if g == CG // 2:
                                load_idx(a, it, c, 1)
                            if g == 0:
                                sp.wait_ge(a.go, 1)
                            sp.wait_ge(a.e_done, it * CG + g + 1)
                            sp.dma_start(ea[0:D, g % KV_RING, :],
                                         ea_in[:, bass.ds(c * (CT * P) + g * (G * P), G * P)]
                                         ).then_inc(a.ea_ready[g % KV_RING], 16)

            def load_sums(k, w):
                sp.wait_ge(sums_whole[k], 1)
                sp.dma_start(agg[:, :, 0:w], rows(sums[k])).then_inc(sums_loaded[k], 16)

            bad = load_bad(sp)
            with sp.If(bad):
                aggregate(0)
                load_sums(0, WA)
            def store_kv(a, b):
                sp.wait_ge(n_ea, b + 2)
                sp.dma_start(rows(kv_tab)[:, 2 * a:2 * b, :], kv_new[:, 2 * a:2 * b, :]).then_inc(s_kv_stored, 16)

            def store_q(a, b, steps):
                sp.wait_ge(n_split, steps)
                sp.dma_start(rows(q_tab)[:, 2 * a:2 * b, :], parts[:, 2 * a:2 * b, 0:3 * D]).then_inc(s_q_stored, 16)

            store_kv(0, 5)
            store_kv(5, 9)
            store_kv(9, 12)
            store_kv(12, NP)
            store_q(0, 8, 4 * SPLIT)
            store_q(8, NP, NP // 2 * SPLIT + 3)
            attention()
            sp.wait_ge(sums_whole[1], 1)
            for half in (slice(0, NP), slice(NP, NB)):
                sp.dma_start(agg[:, half, 0:WT], rows(sums[1])[:, half, :]).then_inc(sums_half[half.start // NP], 16)
            with sp.If(bad):
                sp.wait_ge(s_t2, 1)
                sp.dma_start(rows(t2_tab), ya[:, :, :]).then_inc(s_tab2, 16)
                sp.wait_ge(s_tab2, 16)
                sp.sem_inc(L[2].go, 1)
                aggregate(2)
                load_sums(2, WA)
            with sp.If(bad):
                sp.wait_ge(s_t3, 1)
                sp.dma_start(rows(t3_tab), ya[:, :, :]).then_inc(s_tab3, 16)
                sp.wait_ge(s_tab3, 16)
                sp.sem_inc(L[3].go, 1)
                aggregate(3)
                load_sums(3, WA)
            sp.wait_ge(s_final, 1)
            full = n_nodes // P
            sp.dma_start(out[0:NL * P, :].rearrange("(b p) d -> p b d", p=P), xa[:, 0:NL, :]).then_inc(s_stored, 16)
            sp.wait_ge(s_norm, 4)
            sp.dma_start(out[NL * P:full * P, :].rearrange("(b p) d -> p b d", p=P), xa[:, NL:full, :]).then_inc(s_stored, 16)
            sp.dma_start(out[full * P:n_nodes, :], xa[0:n_nodes - full * P, full, :]).then_inc(s_stored, 16)
            sp.wait_ge(s_stored, 48)

        @block.gpsimd
        def _(pool):
            nc.gpsimd.memset(ident[:, :], 0.0).then_inc(s_pool, 1)
            nc.gpsimd.iota(iota_i[:, :], [[1, P]], base=0, channel_multiplier=0).then_inc(s_pool, 1)
            nc.gpsimd.iota(key_i[:, :], [[1, KEYS]], base=0, channel_multiplier=0).then_inc(s_pool, 1)
            pool.wait_ge(s_pool, 1)
            nc.gpsimd.affine_select(out=ident[:, :], in_=ident[:, :], compare_op=ALU.not_equal, fill=1.0, base=0,
                                    pattern=[[-1, P]], channel_multiplier=1).then_inc(s_ident, 1)
            nc.gpsimd.memset(counts[:, :, :].rearrange("p h n -> p (h n)").bitcast(i32), 0).then_inc(b_clear, 1)
            pool.wait_ge(s_in_x, 16)
            pool.wait_ge(b_clear, 1)
            nc.gpsimd.memset(xT[D:D + 1, :, :], 1.0).then_inc(s_pool_split, 1)
            pool.wait_ge(s_pool_split, 1)
            nc.gpsimd.tensor_copy(parts[:, :, HIGH:HIGH + D], xa[:, :, :]).then_inc(s_pool_split, 1)
            pool.wait_ge(s_pool_split, 2)
            nc.gpsimd.tensor_tensor(ya[:, :, :], xa[:, :, :], parts[:, :, HIGH:HIGH + D],
                                    ALU.subtract).then_inc(s_pool_split, 1)
            pool.wait_ge(s_pool_split, 3)
            nc.gpsimd.tensor_copy(parts[:, :, MID:MID + D], ya[:, :, :]).then_inc(s_pool_split, 1)
            pool.wait_ge(s_pool_split, 4)
            nc.gpsimd.tensor_tensor(parts[:, :, LOW:LOW + D], ya[:, :, :], parts[:, :, MID:MID + D],
                                    ALU.subtract).then_inc(s_pool_split, 1)
            npass = passes(pool)

            def add_window(a, k, w, b, n):
                pool.wait_ge(a.flush_ready, n + 1)
                pool.dma_start(sums[k][bass.ds(b, P), :], flush[:, 0:w], accum_op=ALU.add).then_inc(a.flushed, 16)

            def run(k, table, w_row, w_sum):
                a = L[k]
                if k == 1:
                    pool.wait_ge(s_kv_stored, 16 * KV_PIECES)
                else:
                    pool.wait_ge(a.go, 2 if k else 1)
                with pool.Fori(0, npass) as p:
                    wait_alone(pool, a.pass_ready, p + 1)
                    with pool.Fori(0, C) as c:
                        it = pool.snap(p * C + c)
                        for g in range(CG):
                            h = g // (CG // 2)
                            if g % (CG // 2) == 0:
                                pool.wait_ge(a.idx_ready[h], (it + 1) * 16)
                            wait_alone(pool, a.used, it * CG + g + 2)
                            for j in range(G):
                                col = (g % (CG // 2)) * G + j
                                pool.indirect_dma_start(
                                    kv[:, g % KV_RING, j, 0:w_row], None, table,
                                    bass.IndirectOffsetOnAxis(ap=idx[:, h, col:col + 1], axis=0)
                                    ).then_inc(a.gathered[g % KV_RING], 16)
                            if g == CG - 1:
                                b = pool.value_load(base_i[0:1, bass.ds(c, 1)], min_val=0, max_val=LAST_BASE)
                                add_window(a, k, w_sum, b, p * (C + 1) + c)
                    b = pool.value_load(base_i[0:1, C:C + 1], min_val=0, max_val=LAST_BASE)
                    add_window(a, k, w_sum, b, p * (C + 1) + C)
                pool.wait_ge(a.flushed, npass * (16 * (C + 1)))
                nc.gpsimd.sem_inc(sums_whole[k], 1)

            pool.wait_ge(s_zeroed, 64)
            bad = load_bad(pool)
            with pool.If(bad):
                run(0, x_in, D, WA)
            run(1, kv_tab, 2 * D, WT)
            with pool.If(bad):
                run(2, t2_tab, D, WA)
            with pool.If(bad):
                run(3, t3_tab, D, WA)

        @block.scalar
        def _(act):
            nc.scalar.preload_act_table(ACT.Sqrt)
            act.wait_ge(b_clear, 1)
            act.wait_ge(b_oh, 1)

            def write_window(c, u, first):
                act.wait_ge(b_mm, c + BR + 1)
                act.wait_ge(b_wr, c + BR)
                nc.scalar.copy(counts[:, :, bass.ds(first, SW)],
                               bank[u][:, 0:KEYS].rearrange("p (h n) -> p h n", n=SW)).then_inc(b_wr, 1)

            with act.Fori(0, BC // BR) as i:
                firsts = load_firsts(act, i * BR)
                for w in range(BR):
                    write_window(i * BR + w, w, firsts[w])
            firsts = load_firsts(act, BC // BR * BR)
            for w in range(BC % BR):
                write_window(BC // BR * BR + w, w, firsts[w])

            def dense(m, beside=None):
                def convert(b, u):
                    act.wait_ge(d_mm, b + (m * NH + 1))
                    nc.scalar.copy(block_b[:, u, 0:ACT_H, :], counts[:, 0:ACT_H, bass.ds(b * P, P)]).then_inc(d_ca, 1)

                def evict(b, u):
                    act.wait_ge(d_mm, b + (m * NH + 3))
                    if m == 0:
                        nc.scalar.copy(agg[:, bass.ds(b, 1), 0:WA].rearrange("p o d -> p (o d)"),
                                       N_o[u][:, HIGH:HIGH + WA]).then_inc(d_ea, 1)
                    else:
                        nc.scalar.activation(agg[:, bass.ds(b, 1), 0:D].rearrange("p o d -> p (o d)"),
                                             N_o[u][:, HIGH:HIGH + D], ACT.Copy,
                                             scale=dinv_in[:, bass.ds(b, 1)]).then_inc(d_ea, 1)

                act.wait_ge(d_free, m + 1)
                for b in range(2):
                    convert(b, b)
                with act.Fori(0, NH // 2 - 1) as i:
                    for u in range(2):
                        evict(i * 2 + u, u)
                        convert(i * 2 + (u + 2), u)
                        if beside:
                            beside(i * 2 + u)
                for b in range(NH - 3, NH):
                    evict(b, b % 2)
                    if b + 2 < NH:
                        convert(b + 2, b % 2)
                    if beside:
                        beside(b)

            npass = passes(act)

            def node(m, ins, out2=None):
                def stage(i, u):
                    act.wait_ge(n_tr, i + (m * NP + 1))
                    for k, src in enumerate(ins):
                        if src is agg and m == 0:
                            for q in range(2):
                                last = nc.scalar.activation(xs[:, u, 2 * k + q, :],
                                                            agg[:, bass.ds(i * 2 + q, 1), 0:D].rearrange("p o d -> p (o d)"),
                                                            ACT.Copy, scale=stat[:, 0, bass.ds(i * 2 + q, 1)])
                        else:
                            last = nc.scalar.copy(xs[:, u, 2 * k:2 * k + 2, :], src[:, bass.ds(i * 2, 2), 0:D])
                    last.then_inc(n_staged, 1)

                def copy_transposes(i, u):
                    act.wait_ge(n_tr, i + (m * NP + 3))
                    act.wait_ge(n_mm, i + (m * NP + 1))
                    w = 2 * len(ins) * P
                    nc.scalar.copy(xT[0:D, u, 0:w], N_t[u][0:D, 0:w]).then_inc(n_xT, 1)

                def evict(i, u):
                    if out2 is not None:
                        act.wait_ge(n_mm, i + (m * NP + 3))
                        w = out2.shape[2]
                        nc.scalar.copy(out2[:, bass.ds(i * 2, 2), :],
                                       N_2[u][:, 0:2 * w].rearrange("p (q d) -> p q d", q=2)).then_inc(n_ea, 1)

                act.wait_ge(n_go, m + 1)
                stage(0, 0)
                stage(1, 1)
                copy_transposes(0, 0)
                with act.Fori(0, NP // 2 - 1) as i:
                    for u in range(2):
                        stage(i * 2 + (u + 2), u)
                        copy_transposes(i * 2 + (u + 1), 1 - u)
                        evict(i * 2 + u, u)
                stage(NP - 1, 0)
                for n in (NP - 3, NP - 2):
                    copy_transposes(n + 1, (n + 1) % 2)
                    evict(n, n % 2)
                evict(NP - 1, 0)

            roots = [0]

            def root(ap):
                roots[0] += 1
                act.wait_ge(s_sqrt_in, roots[0])
                nc.scalar.activation(ap, ap, ACT.Sqrt).then_inc(s_sqrt, 1)

            norms = [0]

            def normalise():
                root(stat[:, 2, :])
                norms[0] += 1
                act.wait_ge(s_norm_in, norms[0])
                for b in range(NL, NB):
                    last = nc.scalar.activation(xa[:, b, :], ya[:, b, :], ACT.Identity, bias=stat[:, 1, b:b + 1],
                                                scale=stat[:, 3, b:b + 1])
                last.then_inc(s_norm, 1)

            dense(0)
            bad = load_bad(act)
            root(dinv_in[:, :])
            node(0, [xa, agg])
            normalise()
            node(1, [xa], kv_new)
            a = A
            nc.scalar.preload_act_table(ACT.Exp)
            act.wait_ge(s_kv_stored, 16 * KV_PIECES)
            nc.scalar.copy(ea[D:D + 1, :, :].rearrange("p r n -> p (r n)"),
                           ones[D:D + 1, 0:1].broadcast_to([1, KV_RING * G * P])).then_inc(a.go, 1)
            with act.Fori(0, npass) as p:
                with act.Fori(0, C) as c:
                    it = act.snap(p * C + c)
                    act.wait_ge(a.q_ready, (it + 1) * 16)
                    act.wait_ge(a.q_done, it * CG + 2)
                    nc.scalar.copy(q_win[:, :], q_land[:, :]).then_inc(a.qwin, 1)
                    for g in range(CG):
                        u, n = g % 2, it * CG + g
                        act.wait_ge(a.ohT_ps, n + 3)
                        act.wait_ge(a.q_done, n + 1)
                        nc.scalar.copy(ohT[:, u, :, :].rearrange("p g n -> p (g n)"), T_ps[u][:, 0:G * P]).then_inc(a.ohT_sb, 1)
                        act.wait_ge(a.seg, n + 1)
                        nc.scalar.copy(oh[:, u, :, :].rearrange("p g n -> p (g n)"),
                                       oh_b[:, u, :, :].rearrange("p g n -> p (g n)")).then_inc(a.oh32, 1)
                        act.wait_ge(a.sc, n + 1)
                        nc.scalar.activation(msg[:, u, :, D:WT], sc[:, u, :].rearrange("p (g h) -> p g h", h=H),
                                             ACT.Exp).then_inc(a.exp, 1)
                    act.wait_ge(a.seg, (it + 1) * CG + 2)
                    act.wait_ge(a.flushed, (p * (C + 1) + c + 1) * 16)
                    nc.scalar.copy(flush[:, 0:WT], acc[:, 0:WT]).then_inc(a.flush_ready, 1)
            root(dinv_out[:, :])
            root(stat[:, 2, :])
            norms[0] += 1
            act.wait_ge(s_norm_in, norms[0])
            for b in range(NL, NB):
                last = nc.scalar.activation(agg[:, b, 0:D], ya[:, b, :], ACT.Identity, bias=stat[:, 5, b:b + 1],
                                            scale=stat[:, 4, b:b + 1])
            last.then_inc(s_split_act, 1)
            for part, step in ((HIGH, 1), (MID, 2)):
                for blocks, ready in ((slice(0, NL), step), (slice(NL, NB), step + 1)):
                    if part == HIGH and blocks.start:
                        act.wait_ge(s_split_act, 1)
                    else:
                        act.wait_ge(s_split, ready)
                    nc.scalar.copy(parts[:, blocks, part:part + D], agg[:, blocks, 0:D]).then_inc(s_split_act, 1)

            def norm(b):
                return nc.scalar.activation(xa[:, bass.ds(b, 1), :].rearrange("p o d -> p (o d)"),
                                            ya[:, bass.ds(b, 1), :].rearrange("p o d -> p (o d)"), ACT.Identity,
                                            bias=stat[:, 1, bass.ds(b, 1)], scale=stat[:, 3, bass.ds(b, 1)])

            with act.If(bad):
                with act.Fori(0, NH) as b:
                    norm(b)
            with act.Else():
                dense(1, norm)
            norm(NH).then_inc(s_norm, 1)
            node(2, [agg])
            normalise()
            node(3, [xa], r3)
            with act.If(bad):
                act.nop()
            with act.Else():
                dense(2)
            normalise()

        @block.tensor
        def _(pe):
            pe.wait_ge(s_ident, 1)
            pe.wait_ge(s_prep, 4)
            for m in range(2):
                last = nc.tensor.transpose(bank[m][0:C, 0:P], cmin[:, m * C:(m + 1) * C], ident[:, :])
            last.then_inc(s_prep_pe, 1)
            pe.wait_ge(s_prep, 8)
            for m in range(2):
                last = nc.tensor.transpose(bank[2 + m][:, 0:C], cwide[:, m, :], ident[0:C, 0:C])
            last.then_inc(s_prep_pe, 1)

            pe.wait_ge(s_prep, 15)
            nc.tensor.matmul(bank[4][:, 0:BC], ones[0:1, :], first_f[0:1, :], start=True, stop=True).then_inc(s_prep_pe, 1)
            def window(c, w):
                bank_w = bank[w % BR][:, 0:KEYS]
                pe.wait_ge(b_oh, c + 1)
                pe.wait_ge(b_wr, c + 1)
                for t in range(BT):
                    nc.tensor.matmul(bank_w, lo_oh[:, w // 2, :, (w % 2) * BT + t], key_oh[:, w % BR, t, :],
                                     start=(t == 0), stop=False, skip_group_check=True)
                before = (w - 1) % (2 * BR)
                nc.tensor.matmul(bank_w.rearrange("p (h n) -> p h n", n=SW)[:, :, 0],
                                 lo_oh[:, before // 2, :, (before % 2) * BT + BT - 1],
                                 carry_oh[:, :, bass.ds(c, 1)].rearrange("p h o -> p (h o)"),
                                 start=False, stop=True, skip_group_check=True).then_inc(b_mm, 1)

            with pe.Fori(0, BC // (2 * BR)) as i:
                for w in range(2 * BR):
                    window(i * (2 * BR) + w, w)
            for w in range(BC % (2 * BR)):
                window(BC // (2 * BR) * (2 * BR) + w, w)

            def dense(m):
                if m == 0:
                    pe.wait_ge(s_pool_split, 5)
                pe.wait_ge(d_go, m + 1)

                def product(b, u):
                    n = b + m * NH
                    pe.wait_ge(d_ca, n + 1)
                    pe.wait_ge(d_cv, n + 1)
                    pe.wait_ge(d_ev, n + 1)
                    for h in range(NH):
                        last = nc.tensor.matmul(N_o[u][:, 0:ONE + 1], block_b[:, u, h, :], parts[:, h, 0:ONE + 1],
                                                start=(h == 0), stop=(h == NH - 1))
                    last.then_inc(d_mm, 1)

                with pe.Fori(0, NH // 2) as i:
                    for u in range(2):
                        product(i * 2 + u, u)
                product(NH - 1, 0)

            def out_degrees():
                pe.wait_ge(s_deg_oh, 1)
                nc.tensor.matmul(bank[7][:, 0:NB], zero_b[:, :], zero_b[:, 0:NB], start=True, stop=False,
                                 skip_group_check=True)
                with pe.Fori(0, NT // (2 * G)) as i:
                    for u in range(2):
                        pe.wait_ge(s_deg_oh, i * 2 + u + 2)
                        for j in range(G):
                            last = nc.tensor.matmul(bank[7][:, 0:NB], oh_b[:, u, j, :], oh_hi[:, u, j, :],
                                                    start=False, stop=False, skip_group_check=True)
                        last.then_inc(s_deg_mm, 1)

            npass = passes(pe)

            def aggregate(k):
                a = L[k]
                with pe.Fori(0, npass) as p:
                    with pe.Fori(0, C) as c:
                        it = pe.snap(p * C + c)
                        pe.wait_ge(a.flush_ready, p * (C + 1) + c + 1)
                        for g in range(CG):
                            r = g % KV_RING
                            pe.wait_ge(a.gathered[r], (it * 2 + g // KV_RING + 1) * (16 * G))
                            pe.wait_ge(a.oh_ready, it * CG + g + 1)
                            for j in range(G):
                                last = nc.tensor.matmul(acc[:, 0:WA], oh[:, g % 2, j, :], kv[:, r, j, 0:WA],
                                                        start=(g == 0 and j == 0), stop=(g == CG - 1 and j == G - 1))
                            last.then_inc(a.used, 1)

            def node(m, products):
                ins = 1 + max(k for terms in products for k, _, _ in terms)

                def transposes(i, u):
                    pe.wait_ge(n_staged, i + (m * NP + 1))
                    pe.wait_ge(n_xT, i + (m * NP + 1))
                    for k in range(2 * ins):
                        last = nc.tensor.transpose(N_t[u][0:D, k * P:(k + 1) * P], xs[:, u, k, :], ident[:, :])
                    last.then_inc(n_tr, 1)

                deep = len(products) == 2

                def product(i, u, slot):
                    pe.wait_ge(n_xT, i + (m * NP + 3))
                    if deep:
                        pe.wait_ge(n_ev, i + (m * NP - 1))
                        pe.wait_ge(n_ea, i + (m // 2 * NP + 1))
                    else:
                        pe.wait_ge(n_ev, i + (m * NP + 1))
                    for terms, out_bank in zip(products, ((N_4 if deep else N_o)[slot], N_2[u])):
                        for q in range(2):
                            for j, (k, w, w_rows) in enumerate(terms):
                                n = w.shape[1]
                                last = nc.tensor.matmul(out_bank[:, q * n:(q + 1) * n],
                                                        xT[0:w_rows, u, (2 * k + q) * P:(2 * k + q + 1) * P], w,
                                                        start=(j == 0), stop=(j == len(terms) - 1))
                    last.then_inc(n_mm, 1)

                pe.wait_ge(n_go, m + 1)
                transposes(0, 0)
                ring = 4 if deep else 2
                with pe.Fori(0, NP // ring) as i:
                    for n in range(ring):
                        transposes(i * ring + (n + 1), (n + 1) % 2)
                        product(i * ring + n, n % 2, n)
                product(NP - 1, 0, 0)

            dense(0)
            pe.wait_ge(s_degsum, 1)
            nc.tensor.matmul(bank[4][0:1, 0:1], degsum[:, :], ones[:, 0:1], start=True, stop=True).then_inc(s_total, 1)
            bad = load_bad(pe)
            with pe.If(bad):
                aggregate(0)
            pe.wait_ge(s_in_w, 96)
            node(0, [[(0, w_self_t[:, :], D + 1), (1, w_neigh_t[:, :], D)]])
            node(1, [[(0, w_kvq_t[:, 2 * D:3 * D], D + 1)], [(0, w_kvq_t[:, 0:2 * D], D + 1)]])

            a = A

            def segment(it, g):
                n = it * CG + g
                pe.wait_ge(a.used, n + USED0 + 1)
                pe.wait_ge(a.oh32, n + 3)
                for j in range(G):
                    last = nc.tensor.matmul(acc[:, 0:WT], oh[:, g % 2, j, :], msg[:, g % 2, j, :],
                                            start=(g == 0 and j == 0), stop=(g == CG - 1 and j == G - 1))
                last.then_inc(a.seg, 1)

            pe.wait_ge(n_ea, NP + 2)
            with pe.Fori(0, npass) as p:
                with pe.Fori(0, C) as c:
                    it = pe.snap(p * C + c)
                    for g in range(CG):
                        u, r, n = g % 2, g % KV_RING, it * CG + g
                        pe.wait_ge(a.oh_ready, n + 1)
                        pe.wait_ge(a.ohT_sb, n + 1)
                        for j in range(G):
                            last = nc.tensor.transpose(T_ps[u][:, j * P:(j + 1) * P], oh_b[:, u, j, :], ident_b[:, :])
                        last.then_inc(a.ohT_ps, 1)
                        pe.wait_ge(a.ea_ready[r], (it * 2 + g // KV_RING + 1) * 16)
                        pe.wait_ge(a.t1, n + 1)
                        for j in range(G):
                            last = nc.tensor.matmul(E_ps[u][:, j * D:(j + 1) * D], ea[0:D + 1, r, j * P:(j + 1) * P],
                                                    w_edge_t[:, :], start=True, stop=True)
                        last.then_inc(a.e_done, 1)
                        if g == 0:
                            pe.wait_ge(a.qwin, it + 2)
                        pe.wait_ge(a.ohT_sb, n + 3)
                        pe.wait_ge(a.t2, n + 1)
                        for j in range(G):
                            for part in range(3):
                                last = nc.tensor.matmul(Q_ps[u][:, j * D:(j + 1) * D], ohT[:, u, j, :],
                                                        q_win[:, part * D:(part + 1) * D],
                                                        start=(part == 0), stop=(part == 2))
                        last.then_inc(a.q_done, 1)
                        if g:
                            segment(it, g - 1)
                        else:
                            pe.wait_ge(a.flush_ready, p * (C + 1) + c + 1)
                    segment(it, CG - 1)

            with pe.If(bad):
                out_degrees()
            with pe.If(bad):
                aggregate(2)
            with pe.Else():
                dense(1)
            node(2, [[(0, w_gcn_t[:, :], D + 1)]])
            node(3, [[(0, w_lr_t[:, 0:D], D + 1)], [(0, w_lr_t[:, D:2 * D], D + 1)]])
            with pe.If(bad):
                aggregate(3)
            with pe.Else():
                dense(2)

        @block.vector
        def _(dve):
            class Steps:
                def __init__(self, s, base=0):
                    self.s, self.n, self.base = s, 0, base

                def __call__(self, ins):
                    self.n += 1
                    ins.then_inc(self.s, 1)
                    dve.wait_ge(self.s, self.base + self.n)

            V = nc.vector
            V.memset(agg[:, :, :], 0.0).then_inc(s_zeros, 1)
            for s_ in (n_tr, n_xT, n_mm, n_ev, n_ea):
                V.sem_inc(s_, 2)
            for k in range(4):
                V.sem_inc(L[k].used, USED0)
            V.sem_inc(A.e_done, KV_RING)
            V.sem_inc(A.qwin, 1)
            V.sem_inc(b_wr, BR)
            V.sem_inc(b_mm, BR)
            for s_ in (d_mm, d_ev):
                V.sem_inc(s_, 2)
            for s_ in (A.oh32, A.ohT_ps, A.ohT_sb, A.q_done, A.t1, A.t2, A.seg):
                V.sem_inc(s_, 2)

            prep = Steps(s_prep)
            dve.wait_ge(s_in_e, 32)
            prep(V.tensor_copy(dst_f[:, :], dst_all[:, :]))
            prep(V.tensor_reduce(cmin[:, 0:C], dst_f[:, :].rearrange("p (c t) -> p c t", t=CT), AX, ALU.min))
            prep(V.scalar_tensor_tensor(out=slot0[:, :], in0=dst_f[:, :], scalar=float(PAD_DST), in1=dst_f[:, :],
                                        op0=ALU.is_lt, op1=ALU.mult))
            prep(V.tensor_reduce(cmin[:, C:2 * C], slot0[:, :].rearrange("p (c t) -> p c t", t=CT), AX, ALU.max))
            dve.wait_ge(s_prep_pe, 1)
            prep(V.tensor_reduce(cred[:, 0:1], bank[0][0:C, 0:P], AX, ALU.min))
            prep(V.tensor_reduce(cred[:, 1:2], bank[1][0:C, 0:P], AX, ALU.max))
            for m in range(2):
                prep(V.tensor_copy(cwide[:, m, :], cred[:, m:m + 1].broadcast_to([C, P])))
            dve.wait_ge(s_prep_pe, 2)
            prep(V.tensor_copy(base0[:, :], bank[2][:, 0:C]))
            prep(V.tensor_tensor(span_f[:, :], bank[3][0:1, 0:C], base0[0:1, :], ALU.subtract))
            prep(V.tensor_reduce(span_m[:, :], span_f[:, :], AX, ALU.max))
            prep(V.tensor_tensor(slot0[:, :].rearrange("p (c t) -> p c t", t=CT),
                                 dst_f[:, :].rearrange("p (c t) -> p c t", t=CT),
                                 base0[:, :].unsqueeze(2).broadcast_to([P, C, CT]), ALU.subtract))
            prep(V.memset(base_i[:, :], 0))
            V.tensor_copy(span_i[:, :], span_m[:, :]).then_inc(s_base, 1)
            prep(V.memset(ones[:, :], 1.0))
            prep(V.tensor_scalar(first_f[:, :], dst_f[0:1, :].rearrange("p (c t) -> p c t", t=BT)[:, :, 0], float(n_nodes),
                                 None, ALU.min))
            dve.wait_ge(s_ident, 1)
            prep(V.tensor_copy(ident_b[:, :], ident[:, :]))
            prep(V.tensor_copy(iota_f[:, :], iota_i[:, :]))
            prep(V.tensor_copy(iota_h[:, :], key_i[:, :]))
            prep(V.memset(zero_b[:, :], 0.0))
            prep(V.tensor_scalar(dst_all[:, :], src_all[:, :], P - 1, None, ALU.bitwise_and))
            prep(V.tensor_scalar(src_all[:, :], src_all[:, :], 7, None, ALU.logical_shift_right))
            prep(V.tensor_copy(lo_h[:, :], dst_all[:, :]))
            prep(V.tensor_copy(iota_6[:, :, :], iota_f[:, :].unsqueeze(2).broadcast_to([P, P, 2 * BT])))
            dve.wait_ge(s_prep_pe, 3)
            prep(V.memset(first_i[:, :], 0))
            prep(V.tensor_copy(first_i[:, 0:BC], first_f[:, :]))
            prep(V.tensor_tensor(key[:, :].rearrange("p (c t) -> p c t", t=BT),
                                 dst_f[:, :].rearrange("p (c t) -> p c t", t=BT),
                                 bank[4][:, 0:BC].unsqueeze(2).broadcast_to([P, BC, BT]), ALU.subtract))
            tile_before = dst_f[:, :].rearrange("p (c t) -> p c t", t=BT)[:, 0:BC - 1, BT - 1]
            prep(V.memset(carry[:, :], float(PAD_DST)))
            prep(V.tensor_tensor(carry[:, 1:BC], tile_before, bank[4][:, 1:BC], ALU.not_equal))
            prep(V.scalar_tensor_tensor(out=carry[:, 1:BC], in0=carry[:, 1:BC], scalar=float(PAD_DST),
                                        in1=src_all[:, :].rearrange("p (c t) -> p c t", t=BT)[:, 0:BC - 1, BT - 1],
                                        op0=ALU.mult, op1=ALU.add))
            prep(V.tensor_copy(carry_h[:, :], carry[:, :]))
            prep(V.tensor_scalar(dst_f[:, :], key[:, :], float(SW), float(PAD_DST), ALU.is_ge, ALU.mult))
            prep(V.tensor_tensor(dst_f[:, :], dst_f[:, :], key[:, :], ALU.add))
            prep(V.tensor_scalar(key[:, :], key[:, :], 0.0, float(PAD_DST), ALU.is_lt, ALU.mult))
            prep(V.tensor_tensor(dst_f[:, :], dst_f[:, :], key[:, :], ALU.add))
            prep(V.scalar_tensor_tensor(out=key[:, :], in0=src_all[:, :], scalar=float(SW), in1=dst_f[:, :],
                                        op0=ALU.mult, op1=ALU.add))

            def onehot(dst, width, vals, at):
                return V.tensor_tensor(dst, iota_f[:, 0:width].unsqueeze(1).broadcast_to([P, G, width]),
                                       vals[:, bass.ds(at, G)].unsqueeze(2).broadcast_to([P, G, width]), ALU.is_equal)

            def window_onehots(c, w):
                dve.wait_ge(b_mm, c + 1)
                if w % 2 == 0:
                    V.tensor_tensor(lo_oh[:, w // 2, :, :], iota_6[:, :, :],
                                    lo_h[:, bass.ds(c * BT, 2 * BT)].unsqueeze(1).broadcast_to([P, P, 2 * BT]), ALU.is_equal)
                for t in range(BT):
                    last = V.tensor_scalar(key_oh[:, w % BR, t, :], iota_h[:, :], key[:, bass.ds(c * BT + t, 1)], None,
                                           ALU.is_equal)
                last.then_inc(b_oh, 1)

            st = prep
            st(V.memset(lo_oh[:, BR - 1, :, :], 0.0))
            for h in range(NH):
                last = V.tensor_scalar(carry_oh[:, h, :], carry_h[:, :], float(h), None, ALU.is_equal)
            st(last)
            dve.wait_ge(b_clear, 1)
            with dve.Fori(0, BC // (2 * BR)) as i:
                for w in range(2 * BR):
                    window_onehots(i * (2 * BR) + w, w)
            for w in range(BC % (2 * BR)):
                window_onehots(BC // (2 * BR) * (2 * BR) + w, w)
            dve.wait_ge(b_wr, BC + BR)

            def dense(m, tail=None):
                def convert(b, u):
                    dve.wait_ge(d_mm, b + (m * NH + 1))
                    V.tensor_copy(block_b[:, u, ACT_H:NH, :], counts[:, ACT_H:NH, bass.ds(b * P, P)]).then_inc(d_cv, 1)

                def evict(b, u):
                    n = b + m * NH
                    row = agg[:, bass.ds(b, 1), 0:D].rearrange("p o d -> p (o d)")
                    dve.wait_ge(d_mm, n + 3)
                    dve.wait_ge(d_ea, n + 1)
                    scale = dinv_in[:, bass.ds(b, 1)] if m else 1.0
                    V.scalar_tensor_tensor(out=row, in0=N_o[u][:, MID:MID + D], scalar=scale, in1=row,
                                           op0=ALU.mult, op1=ALU.add).then_inc(d_st, 1)
                    dve.wait_ge(d_st, n + 1)
                    V.scalar_tensor_tensor(out=row, in0=N_o[u][:, LOW:LOW + D], scalar=scale, in1=row,
                                           op0=ALU.mult, op1=ALU.add).then_inc(d_ev, 1)

                def step(b, u, more=True):
                    evict(b, u)
                    if more:
                        convert(b + 2, u)
                    if tail:
                        tail(b, b + m * NH)

                V.sem_inc(d_free, 1)
                for b in range(2):
                    convert(b, b)
                V.sem_inc(d_go, 1)
                with dve.Fori(0, NH // 2 - 1) as i:
                    for u in range(2):
                        step(i * 2 + u, u)
                for b in range(NH - 3, NH):
                    step(b, b % 2, b + 2 < NH)
                dve.wait_ge(d_ev, (m + 1) * NH + 2)

            def out_degrees():
                st = Steps(deg_step)
                st(V.tensor_copy(lo_f[:, :], dst_all[:, :]))
                st(V.tensor_scalar(slot[:, :], slot0[:, :], float(n_nodes), float(PAD_DST), ALU.is_ge, ALU.mult))
                st(V.tensor_tensor(slot[:, :], slot[:, :], src_all[:, :], ALU.add))
                V.sem_inc(s_deg_oh, 1)
                V.sem_inc(s_deg_mm, 2)
                with dve.Fori(0, NT // (2 * G)) as i:
                    for u in range(2):
                        dve.wait_ge(s_deg_mm, i * 2 + u + 1)
                        onehot(oh_b[:, u, :, :], P, lo_f, (i * 2 + u) * G)
                        onehot(oh_hi[:, u, :, :], NB, slot, (i * 2 + u) * G).then_inc(s_deg_oh, 1)
                dve.wait_ge(s_deg_mm, NT // G + 2)
                st(V.tensor_scalar(outdeg[:, :], bank[7][:, 0:NB], 1.0, None, ALU.max))

            npass = passes(dve)

            def start_pass_state(k):
                a = L[k]
                st = Steps(a.step)
                st(V.tensor_copy(slot[:, :], slot0[:, :]))
                st(V.tensor_copy(base_f[:, :], base0[0:1, :]))
                return st

            def open_pass(k, p):
                a = L[k]
                st = Steps(a.step, p * 4 + (2 if k == 1 else 3))
                st(V.tensor_scalar(base_i[0:1, 1:C + 1], base_f[:, :], float(LAST_BASE), None, ALU.min))
                st(V.memset(flush[:, :], 0.0))
                V.sem_inc(a.pass_ready, 1)
                V.sem_inc(a.flush_ready, 1)

            def close_pass(k, p):
                dve.wait_ge(L[k].flushed, (p + 1) * (16 * (C + 1)))
                st = Steps(L[k].step, p * 4 + (4 if k == 1 else 5))
                st(V.tensor_scalar(slot[:, :], slot[:, :], float(-P), None, ALU.add))
                st(V.tensor_scalar(base_f[:, :], base_f[:, :], float(P), None, ALU.add))

            def copy_window(a, p, c, n, w):
                dve.wait_ge(a.flushed, (p * (C + 1) + c + 1) * 16)
                V.tensor_copy(flush[:, 0:w], acc[:, 0:w]).then_inc(a.flush_ready, 1)

            def aggregate(k):
                a = L[k]
                pass_state = start_pass_state(k)
                pass_state(V.memset(kv[:, :, :, D:WA], 1.0))
                V.sem_inc(a.go, 1)
                with dve.Fori(0, npass) as p:
                    open_pass(k, p)
                    with dve.Fori(0, C) as c:
                        it = dve.snap(p * C + c)
                        for g in range(CG):
                            dve.wait_ge(a.used, it * CG + g + KV_RING)
                            onehot(oh[:, g % 2, :, :], P, slot, c * CT + g * G).then_inc(a.oh_ready, 1)
                        dve.wait_ge(a.used, (it + 1) * CG + USED0)
                        copy_window(a, p, c, it, WA)
                    close_pass(k, p)

            roots = [0]

            def root(ins):
                roots[0] += 1
                ins.then_inc(s_sqrt_in, 1)
                dve.wait_ge(s_sqrt, roots[0])

            norms = [0]

            def deviations(y):
                even, odd = bn[:, :, 1], bn[:, :, 4]
                st(V.tensor_tensor(stat[:, 1, :], even, odd, ALU.subtract))
                st(V.tensor_tensor(stat[:, 1, :], stat[:, 1, :], stat[:, 1, :], ALU.mult))
                st(V.scalar_tensor_tensor(out=stat[:, 1, :], in0=stat[:, 1, :], scalar=D / 4, in1=bn[:, :, 2],
                                          op0=ALU.mult, op1=ALU.add))
                st(V.tensor_tensor(stat[:, 1, :], stat[:, 1, :], bn[:, :, 5], ALU.add))
                roots[0] += 1
                V.tensor_scalar(stat[:, 2, :], stat[:, 1, :], 1.0 / D, 1e-5, ALU.mult, ALU.add).then_inc(s_sqrt_in, 1)
                st(V.tensor_tensor(stat[:, 0, :], even, odd, ALU.add))
                st(V.tensor_scalar(stat[:, 0, :], stat[:, 0, :], 0.5, None, ALU.mult))
                st(V.tensor_tensor(y[:, 0:NL, :], y[:, 0:NL, :], stat[:, 0, 0:NL].unsqueeze(2).broadcast_to([P, NL, D]),
                                   ALU.subtract))
                dve.wait_ge(s_sqrt, roots[0])
                st(V.reciprocal(stat[:, 3, :], stat[:, 2, :]))
                st(V.scalar_tensor_tensor(out=stat[:, 1, :], in0=stat[:, 0, :], scalar=-1.0, in1=stat[:, 3, :],
                                          op0=ALU.mult, op1=ALU.mult))

            def layer_norm(y, dst, dst_ready=None):
                deviations(y)
                V.sem_inc(s_norm_in, 1)
                ins = V.tensor_tensor(dst[:, 0:NL, :], y[:, 0:NL, :],
                                      stat[:, 3, 0:NL].unsqueeze(2).broadcast_to([P, NL, D]), ALU.mult)
                if dst_ready is not None:
                    ins.then_inc(dst_ready, 1)
                else:
                    st(ins)
                    norms[0] += 1
                    dve.wait_ge(s_norm, norms[0])

            def node(m, evict):
                with dve.Fori(0, NP // 2) as i:
                    for u in range(2):
                        dve.wait_ge(n_mm, i * 2 + (u + m * NP + 3))
                        evict(i * 2 + u, N_o[u])
                dve.wait_ge(n_mm, NP - 1 + m * NP + 3)
                evict(NP - 1, N_o[0])

            def pair(ps):
                return ps[:, 0:2 * D].rearrange("p (q d) -> p q d", q=2)

            def residual(m):
                def evict(i, ps):
                    V.tensor_tensor(ya[:, bass.ds(i * 2, 2), :], xa[:, bass.ds(i * 2, 2), :], pair(ps),
                                    ALU.add).then_inc(n_ev, 1)
                    dve.wait_ge(n_ev, i + (m * NP + 3))
                    for q in range(2):
                        last = V.bn_stats(bn[:, bass.ds(i * 2 + q, 1), :].rearrange("p o n -> p (o n)"),
                                          blk(ya, i * 2 + q))
                    last.then_inc(n_bn, 1)

                node(m, evict)
                dve.wait_ge(n_bn, (m // 2 + 1) * NP)

            def split_products(m, base, first):
                def quad(i, pairs, banks):
                    blocks = bass.ds(i * 2, 2 * pairs)
                    left = agg[:, blocks, 0:D]
                    for u in range(pairs):
                        dve.wait_ge(n_mm, i + (m * NP + u + 3))
                    n = first(i, pairs, blocks, left, banks)
                    V.tensor_copy(parts[:, blocks, MID:MID + D], left).then_inc(n_split, 1)
                    dve.wait_ge(n_split, n + 1)
                    V.tensor_tensor(parts[:, blocks, LOW:LOW + D], left, parts[:, blocks, MID:MID + D],
                                    ALU.subtract).then_inc(n_split, 1)

                with dve.Fori(0, NP // 4) as j:
                    for h in range(2):
                        quad(j * 4 + 2 * h, 2, N_4[2 * h:2 * h + 2])
                quad(NP - 1, 1, N_4)
                dve.wait_ge(n_split, base)

            st = Steps(n_step)

            def blk(t, b, w=D):
                return t[:, bass.ds(b, 1), 0:w].rearrange("p o d -> p (o d)")

            def wide(t):
                return t.unsqueeze(2).broadcast_to([P, NB, D])

            def scaled_edge_sums(k):
                aggregate(k)
                dve.wait_ge(sums_loaded[k], 16)
                V.tensor_tensor(agg[:, :, 0:D], agg[:, :, 0:D], wide(dinv_in[:, :]), ALU.mult).then_inc(s_scaled, 1)
                dve.wait_ge(s_scaled, k - 1)

            dve.wait_ge(s_zeroed, 64)
            st(V.memset(agg[:, NH:NB, :], 0.0))
            st(V.memset(parts[:, :, ONE:ONE + 1], 1.0))
            dense(0)
            V.reduce_sum(degsum[:, :], agg[:, :, D:WA].rearrange("p b o -> p (b o)"), AX).then_inc(s_degsum, 1)
            dve.wait_ge(s_total, 1)
            st(V.tensor_scalar(bad_f[:, :], bank[4][0:1, 0:1], float(n_edges), None, ALU.not_equal))
            V.tensor_copy(bad_i[:, :], bad_f[:, :]).then_inc(s_bad, 1)
            bad = load_bad(dve)
            with dve.If(bad):
                aggregate(0)
                dve.wait_ge(sums_loaded[0], 16)
            st(V.tensor_scalar(indeg[:, :], agg[:, :, D:WA].rearrange("p b o -> p (b o)"), 1.0, None, ALU.max))
            st(V.reciprocal(stat[:, 0, :], indeg[:, :]))
            dve.wait_ge(s_in_x, 16)
            dve.wait_ge(s_pool_split, 5)
            V.sem_inc(n_go, 1)
            root(V.tensor_copy(dinv_in[:, :], indeg[:, :]))
            st(V.reciprocal(dinv_in[:, :], dinv_in[:, :]))
            residual(0)
            layer_norm(ya[:, :, :], xa[:, :, :])
            V.sem_inc(n_go, 1)

            def split_queries(i, pairs, blocks, left, banks):
                n = i * (SPLIT // 2)
                for u in range(pairs):
                    V.tensor_scalar(parts[:, bass.ds((i + u) * 2, 2), HIGH:HIGH + D], pair(banks[u]), QSCALE, None,
                                    ALU.mult).then_inc(n_split, 1)
                for u in range(pairs):
                    two = bass.ds((i + u) * 2, 2)
                    dve.wait_ge(n_split, n + (u + 1))
                    V.scalar_tensor_tensor(out=agg[:, two, 0:D], in0=pair(banks[u]), scalar=QSCALE,
                                           in1=parts[:, two, HIGH:HIGH + D], op0=ALU.mult,
                                           op1=ALU.subtract).then_inc(n_ev, 1)
                dve.wait_ge(n_ev, i + (NP + pairs + 2))
                return n + pairs

            Q_STEPS = NP // 2 * SPLIT + 3
            split_products(1, Q_STEPS, split_queries)

            a = A
            start_pass_state(1)

            def scores(it, g):
                u, r, n = g % 2, g % KV_RING, it * CG + g
                dve.wait_ge(a.e_done, n + KV_RING + 1)
                dve.wait_ge(a.gathered[r], (it * 2 + g // KV_RING + 1) * (16 * G))
                pr = prod[:, u, :].rearrange("p (g d) -> p g d", g=G)
                V.tensor_tensor(pr, kv[:, r, :, 0:D], E_ps[u][:, 0:G * D].rearrange("p (g d) -> p g d", g=G),
                                ALU.mult).then_inc(a.t1, 1)

            def reduce_scores(it, g):
                u, n = g % 2, it * CG + g
                dve.wait_ge(a.q_done, n + 3)
                dve.wait_ge(a.t1, n + 3)
                V.tensor_tensor(prod[:, u, :], prod[:, u, :], Q_ps[u][:, 0:G * D], ALU.mult).then_inc(a.t2, 1)
                dve.wait_ge(a.t2, n + 3)
                V.tensor_reduce(sc[:, u, :], prod[:, u, :].rearrange("p (s d) -> p s d", d=HD), AX,
                                ALU.add).then_inc(a.red, 1)
                dve.wait_ge(a.red, n + 1)
                V.tensor_scalar(sc[:, u, :], sc[:, u, :], -5.0, 5.0, ALU.max, ALU.min).then_inc(a.sc, 1)

            def messages(it, g):
                u, r, n = g % 2, g % KV_RING, it * CG + g
                dve.wait_ge(a.exp, n + 1)
                w = msg[:, u, :, D:WT].unsqueeze(3).broadcast_to([P, G, H, HD])
                V.tensor_tensor(msg[:, u, :, 0:D].rearrange("p g (h d) -> p g h d", h=H),
                                kv[:, r, :, D:2 * D].rearrange("p g (h d) -> p g h d", h=H), w,
                                ALU.mult).then_inc(a.used, 1)

            def slots(it, c, g):
                n = it * CG + g
                dve.wait_ge(a.ohT_ps, n + 1)
                dve.wait_ge(a.oh32, n + 1)
                onehot(oh_b[:, g % 2, :, :], P, slot, c * CT + g * G).then_inc(a.oh_ready, 1)

            PIECES = 3
            SLICE = -(-n_nodes // (C * PIECES))

            def out_degree_piece(p, c, k):
                V.tensor_reduce(outpart[:, :], counts[:, :, bass.ds(c * (PIECES * SLICE) + k * SLICE, SLICE)], AX,
                                ALU.add).then_inc(s_outdeg, 1)
                dve.wait_ge(s_outdeg, p * (2 * PIECES * C + 1) + c * (2 * PIECES) + (2 * k + 2))
                V.tensor_tensor(outdeg[:, 0:NH], outdeg[:, 0:NH], outpart[:, :], ALU.add).then_inc(s_outdeg, 1)

            with dve.Fori(0, npass) as p:
                open_pass(1, p)
                V.memset(outdeg[:, :], 0.0).then_inc(s_outdeg, 1)
                with dve.Fori(0, C) as c:
                    it = dve.snap(p * C + c)
                    slots(it, c, 0)
                    for g in range(CG):
                        scores(it, g)
                        if g:
                            messages(it, g - 1)
                        if g + 1 < CG:
                            slots(it, c, g + 1)
                        if 1 <= g <= PIECES:
                            out_degree_piece(p, c, g - 1)
                        reduce_scores(it, g)
                    messages(it, CG - 1)
                close_pass(1, p)

            with dve.If(bad):
                out_degrees()
            root(V.tensor_scalar(dinv_out[:, :], outdeg[:, :], 1.0, None, ALU.max))
            st(V.reciprocal(dinv_out[:, :], dinv_out[:, :]))
            for part, half in enumerate((slice(0, NP), slice(NP, NB))):
                dve.wait_ge(sums_half[part], 16)
                values, weights = agg[:, half, 0:D], agg[:, half, D:WT]
                st(V.tensor_scalar(weights, weights, 1e-6, None, ALU.add))
                st(V.reciprocal(weights, weights))
                values4 = values.rearrange("p b (h d) -> p b h d", h=H)
                st(V.tensor_tensor(values4, values4, weights.unsqueeze(3).broadcast_to([P, NP, H, HD]), ALU.mult))
                st(V.tensor_tensor(ya[:, half, :], values, xa[:, half, :], ALU.add))
                for b in range(half.start, half.stop):
                    last = V.bn_stats(bn[:, b, :], ya[:, b, :])
                st(last)
            deviations(ya[:, :, :])
            st(V.tensor_tensor(stat[:, 4, :], stat[:, 3, :], dinv_out[:, :], ALU.mult))
            st(V.tensor_tensor(stat[:, 5, :], stat[:, 1, :], dinv_out[:, :], ALU.mult))
            st(V.memset(stat[:, 1, 0:NL], 0.0))
            V.sem_inc(s_norm_in, 1)
            norms[0] += 1
            first, second = agg[:, 0:NL, 0:D], agg[:, NL:NB, 0:D]
            V.tensor_tensor(first, ya[:, 0:NL, :], stat[:, 4, 0:NL].unsqueeze(2).broadcast_to([P, NL, D]),
                            ALU.mult).then_inc(s_split, 1)
            dve.wait_ge(s_split_act, 2)
            V.tensor_tensor(first, first, parts[:, 0:NL, HIGH:HIGH + D], ALU.subtract).then_inc(s_split, 1)
            dve.wait_ge(s_split_act, 3)
            V.tensor_tensor(second, second, parts[:, NL:NB, HIGH:HIGH + D], ALU.subtract).then_inc(s_split, 1)
            dve.wait_ge(s_split_act, 4)
            V.tensor_tensor(parts[:, 0:NL, LOW:LOW + D], first, parts[:, 0:NL, MID:MID + D],
                            ALU.subtract).then_inc(s_split, 1)
            dve.wait_ge(s_split_act, 5)
            V.tensor_tensor(parts[:, NL:NB, LOW:LOW + D], second, parts[:, NL:NB, MID:MID + D],
                            ALU.subtract).then_inc(s_split, 1)
            dve.wait_ge(s_split, 5)
            st(V.memset(agg[:, NH:NB, :], 0.0))

            with dve.If(bad):
                dve.wait_ge(s_norm, norms[0])
                V.tensor_tensor(ya[:, :, :], xa[:, :, :], wide(dinv_out[:, :]), ALU.mult).then_inc(s_t2, 1)
                dve.wait_ge(s_t2, 1)
                scaled_edge_sums(2)
            with dve.Else():
                dense(1)
            dve.wait_ge(s_norm, norms[0])
            V.sem_inc(n_go, 1)
            residual(2)
            layer_norm(ya[:, :, :], xa[:, :, :])
            V.sem_inc(n_go, 1)

            def split_linear(i, pairs, blocks, left, banks):
                n = i * (SPLIT // 2) + Q_STEPS
                for u in range(pairs):
                    two = bass.ds((i + u) * 2, 2)
                    V.tensor_tensor(ya[:, two, :], pair(banks[u]), dinv_in[:, two].unsqueeze(2).broadcast_to([P, 2, D]),
                                    ALU.mult).then_inc(n_ev, 1)
                dve.wait_ge(n_ev, i + (3 * NP + pairs + 2))
                V.tensor_copy(parts[:, blocks, HIGH:HIGH + D], ya[:, blocks, :]).then_inc(n_split, 1)
                dve.wait_ge(n_split, n + 1)
                V.tensor_tensor(left, ya[:, blocks, :], parts[:, blocks, HIGH:HIGH + D], ALU.subtract).then_inc(n_split, 1)
                dve.wait_ge(n_split, n + 2)
                return n + 2

            split_products(3, Q_STEPS + NP // 2 * SPLIT + 4, split_linear)
            st(V.memset(agg[:, NH:NB, :], 0.0))
            dve.wait_ge(n_ea, 2 * NP + 2)
            V.sem_inc(s_t3, 1)

            def residual3(b, n, dense_row=True):
                t = (n - 2 * NH) * 3
                row = blk(ya, b)
                if dense_row:
                    dve.wait_ge(d_ev, n + 3)
                V.tensor_tensor(row, blk(agg, b), blk(r3, b), ALU.add).then_inc(d_tail, 1)
                dve.wait_ge(d_tail, t + 1)
                V.scalar_tensor_tensor(out=row, in0=row, scalar=0.0, in1=blk(xa, b), op0=ALU.max,
                                       op1=ALU.add).then_inc(d_tail, 1)
                dve.wait_ge(d_tail, t + 2)
                V.bn_stats(bn[:, bass.ds(b, 1), :].rearrange("p o n -> p (o n)"), row).then_inc(d_tail, 1)

            with dve.If(bad):
                scaled_edge_sums(3)
                for b in range(NH):
                    residual3(b, 2 * NH + b, dense_row=False)
            with dve.Else():
                dense(2, tail=residual3)
            dve.wait_ge(d_tail, 3 * NH)
            layer_norm(ya[:, :, :], xa[:, :, :], s_final)


def kernel(x, src, dst, edge_attr_96, L0_gnn_W_self, L0_gnn_W_neigh, L0_gnn_b, L1_gnn_Wq, L1_gnn_bq, L1_gnn_Wk, L1_gnn_bk,
           L1_gnn_We, L1_gnn_be, L1_gnn_Wv, L1_gnn_bv, L2_gnn_weight, L2_gnn_bias, L3_gnn_W_lin, L3_gnn_b_lin,
           L3_gnn_W_root, L3_gnn_b_root):
    import numpy as np
    import concourse.bacc as bacc
    from concourse import mybir as mb
    from concourse.bass_utils import run_bass_kernel_spmd

    P, NR, NT, E, N = 128, 26 * 128, 810, 103125, 3125
    A = np.asarray

    def edges(a, fill):
        padded = np.full((NT * P,), fill, np.int32)
        padded[:E] = A(a)
        return np.ascontiguousarray(padded.reshape(NT, P).T)

    def with_bias(w, b):
        return np.ascontiguousarray(np.concatenate([A(w), A(b)[None, :]], axis=0))

    x_pad = np.zeros((NR, 96), np.float32)
    x_pad[:N] = A(x)
    ea_t = np.zeros((96, NT * P), np.float32)
    ea_t[:, :E] = A(edge_attr_96).T
    arrays = {
        "x_in": x_pad,
        "src_in": edges(src, 0),
        "dst_in": edges(dst, 1 << 20),
        "ea_in": ea_t,
        "w_self": with_bias(L0_gnn_W_self, L0_gnn_b),
        "w_neigh": np.ascontiguousarray(A(L0_gnn_W_neigh)),
        "w_kvq": np.concatenate([with_bias(L1_gnn_Wk, L1_gnn_bk), with_bias(L1_gnn_Wv, L1_gnn_bv),
                                 with_bias(L1_gnn_Wq, L1_gnn_bq)], axis=1),
        "w_edge": with_bias(L1_gnn_We, L1_gnn_be),
        "w_gcn": with_bias(L2_gnn_weight, L2_gnn_bias),
        "w_lin_root": np.concatenate([with_bias(A(L3_gnn_W_lin).T, L3_gnn_b_lin),
                                      with_bias(A(L3_gnn_W_root).T, L3_gnn_b_root)], axis=1),
    }
    nc = bacc.Bacc("TRN2", target_bir_lowering=False, num_devices=1)
    args = [nc.dram_tensor(n, list(a.shape), mb.dt.from_np(a.dtype), kind="ExternalInput").ap() for n, a in arrays.items()]
    out = nc.dram_tensor("out", [N, 96], mb.dt.float32, kind="ExternalOutput").ap()
    residual_gnn_kernel(nc, *args, out, N, E)
    r = run_bass_kernel_spmd(nc, [arrays], core_ids=[0])
    return r.results[0]["out"]
```
